# Optimizing a Trainium2 kernel written in Bass

```python
import numpy as np
import jax
import jax.numpy as jnp

def _softmax(x, axis=-1):
    return jax.nn.softmax(x, axis=axis)

def _gelu(x):
    return jax.nn.gelu(x, approximate=True)

def _silu(x):
    return jax.nn.silu(x)

def _sigmoid(x):
    return jax.nn.sigmoid(x)

def _layernorm(x, axis=-1, eps=1e-05):
    m = jnp.mean(x, axis=axis, keepdims=True)
    v = jnp.var(x, axis=axis, keepdims=True)
    return (x - m) / jnp.sqrt(v + eps)

def _scatter_add(tgt, idx, src, axis=0):
    return tgt.at[idx].add(src)

def _segment_sum(src, seg, n):
    return jax.ops.segment_sum(src, seg, n)
kernel_name = 'mk_xattn_ffn_d1_seqx_r2_7f987c'

def setup_inputs(seed: int=0):
    np.random.seed(seed)
    _w = jnp.asarray

    def _rec_inputs():
        import jax
        import jax.numpy as jnp
        _rk = jax.random.key(seed)
        x = 7.22e-05 + 1 * jax.random.normal(jax.random.fold_in(_rk, 1), (8, 512, 512), jnp.float32)
        _lenS = 512 - jax.random.randint(jax.random.fold_in(_rk, 7), (8,), 0, max(1, 512 // 4) + 1, jnp.int32)
        _lenS2 = 77 - jax.random.randint(jax.random.fold_in(_rk, 8), (8,), 0, max(1, 77 // 4) + 1, jnp.int32)
        _ctx_1024P = jax.random.normal(jax.random.fold_in(_rk, 11), (8, 16, 512), jnp.float32)
        _ctx_1024c = jax.random.dirichlet(jax.random.fold_in(_rk, 511), 0.3 * jnp.ones((16,), jnp.float32), (8, 77))
        _ctx_1024t = jnp.einsum('bsk,bkd->bsd', _ctx_1024c, _ctx_1024P)
        _ctx_1024t = _ctx_1024t * jax.lax.rsqrt(jnp.mean(jnp.square(_ctx_1024t)) + 1e-12) * 0.953939
        ctx_1024 = 4.13588e-05 + 0.999923 * (_ctx_1024t + 0.3 * jax.random.normal(jax.random.fold_in(_rk, 611), (8, 77, 512), jnp.float32))
        return (x, ctx_1024, _lenS2)
    x, ctx_1024, _lenS2 = _rec_inputs()

    def _L0_xattn_setup():
        import jax, jax.numpy as jnp
        import numpy as np
        B, N, D, H = (4, 1024, 512, 16)
        DH = D // H
        key = jax.random.key(seed)
        ks = jax.random.split(key, 8)
        scale = 1.0 / np.sqrt(D)
        return {'Q': jax.random.normal(ks[0], (B, N, D), dtype=jnp.float32), 'K': jax.random.normal(ks[1], (B, N, D), dtype=jnp.float32), 'V': jax.random.normal(ks[2], (B, N, D), dtype=jnp.float32), 'valid_lens': jax.random.randint(ks[3], (B,), 1, N, dtype=jnp.int32), 'Wq': jax.random.normal(ks[4], (D, D), dtype=jnp.float32) * scale, 'Wk': jax.random.normal(ks[5], (D, D), dtype=jnp.float32) * scale, 'Wv': jax.random.normal(ks[6], (D, D), dtype=jnp.float32) * scale, 'Wo': jax.random.normal(ks[7], (D, D), dtype=jnp.float32) * scale}
    _L0_xattn_all = _L0_xattn_setup()
    _L0_xattn_in = {k: v for k, v in _L0_xattn_all.items() if k in ('Wq', 'Wk', 'Wv', 'Wo')}
    del _L0_xattn_all

    def _L0_ffn_setup():
        import jax, jax.numpy as jnp
        import numpy as np
        E, TOPK, R = (8, 2, 16)
        D, H, GH = (512, 16, 128)
        HD = D // H
        SCALE = HD ** (-0.5)

        def _svd_moe(x, Wm, U, S, V, b, idx, gates):
            main = jnp.einsum('bsd,od->bso', x, Wm)
            Ug, Sg, Vg = (U[idx], S[idx], V[idx])
            xv = jnp.einsum('bsd,bkrd->bksr', x, Vg)
            xvs = xv * Sg[:, :, None, :]
            eo = jnp.einsum('bksr,bkor->bkso', xvs, Ug)
            expert = jnp.einsum('bkso,bk->bso', eo, gates)
            return main + expert + b
        key = jax.random.key(seed)
        ks = jax.random.split(key, 32)
        B, S = (32, 257)
        inp = {'hidden_states': jax.random.normal(ks[0], (B, S, D), jnp.float32)}
        inp['gw1'] = jax.random.normal(ks[1], (GH, D), jnp.float32) * 0.02
        inp['gb1'] = jnp.zeros((GH,), jnp.float32)
        inp['gw2'] = jax.random.normal(ks[2], (E, GH), jnp.float32) * 0.02
        inp['gb2'] = jnp.zeros((E,), jnp.float32)
        i = 3
        for p in ('q', 'k', 'v', 'o'):
            inp[p + 'Wm'] = jax.random.normal(ks[i], (D, D), jnp.float32) * 0.02
            i += 1
            inp[p + 'U'] = jax.random.normal(ks[i], (E, D, R), jnp.float32) * 0.02
            i += 1
            inp[p + 'S'] = jax.random.normal(ks[i], (E, R), jnp.float32) * 0.1
            i += 1
            inp[p + 'V'] = jax.random.normal(ks[i], (E, R, D), jnp.float32) * 0.02
            i += 1
            inp[p + 'b'] = jnp.zeros((D,), jnp.float32)
        return inp
    _L0_ffn_all = _L0_ffn_setup()
    _L0_ffn_in = {k: v for k, v in _L0_ffn_all.items() if k in ('gw1', 'gb1', 'gw2', 'gb2', 'qWm', 'qU', 'qS', 'qV', 'qb', 'kWm', 'kU', 'kS', 'kV', 'kb', 'vWm', 'vU', 'vS', 'vV', 'vb', 'oWm', 'oU', 'oS', 'oV', 'ob')}
    del _L0_ffn_all
    return {'x': x, 'ctx_1024': ctx_1024, '_lenS2': _lenS2, 'L0_xattn_Wq': _L0_xattn_in['Wq'], 'L0_xattn_Wk': _L0_xattn_in['Wk'], 'L0_xattn_Wv': _L0_xattn_in['Wv'], 'L0_xattn_Wo': _L0_xattn_in['Wo'], 'L0_ffn_gw1': _L0_ffn_in['gw1'], 'L0_ffn_gb1': _L0_ffn_in['gb1'], 'L0_ffn_gw2': _L0_ffn_in['gw2'], 'L0_ffn_gb2': _L0_ffn_in['gb2'], 'L0_ffn_qWm': _L0_ffn_in['qWm'], 'L0_ffn_qU': _L0_ffn_in['qU'], 'L0_ffn_qS': _L0_ffn_in['qS'], 'L0_ffn_qV': _L0_ffn_in['qV'], 'L0_ffn_qb': _L0_ffn_in['qb'], 'L0_ffn_kWm': _L0_ffn_in['kWm'], 'L0_ffn_kU': _L0_ffn_in['kU'], 'L0_ffn_kS': _L0_ffn_in['kS'], 'L0_ffn_kV': _L0_ffn_in['kV'], 'L0_ffn_kb': _L0_ffn_in['kb'], 'L0_ffn_vWm': _L0_ffn_in['vWm'], 'L0_ffn_vU': _L0_ffn_in['vU'], 'L0_ffn_vS': _L0_ffn_in['vS'], 'L0_ffn_vV': _L0_ffn_in['vV'], 'L0_ffn_vb': _L0_ffn_in['vb'], 'L0_ffn_oWm': _L0_ffn_in['oWm'], 'L0_ffn_oU': _L0_ffn_in['oU'], 'L0_ffn_oS': _L0_ffn_in['oS'], 'L0_ffn_oV': _L0_ffn_in['oV'], 'L0_ffn_ob': _L0_ffn_in['ob']}

def reference(x, ctx_1024, _lenS2, L0_xattn_Wq, L0_xattn_Wk, L0_xattn_Wv, L0_xattn_Wo, L0_ffn_gw1, L0_ffn_gb1, L0_ffn_gw2, L0_ffn_gb2, L0_ffn_qWm, L0_ffn_qU, L0_ffn_qS, L0_ffn_qV, L0_ffn_qb, L0_ffn_kWm, L0_ffn_kU, L0_ffn_kS, L0_ffn_kV, L0_ffn_kb, L0_ffn_vWm, L0_ffn_vU, L0_ffn_vS, L0_ffn_vV, L0_ffn_vb, L0_ffn_oWm, L0_ffn_oU, L0_ffn_oS, L0_ffn_oV, L0_ffn_ob):
    import jax
    import jax.numpy as jnp

    def _L0_xattn_ref(Q, K, V, valid_lens, Wq, Wk, Wv, Wo):
        import jax, jax.numpy as jnp
        import numpy as np
        B, N, D, H = (4, 1024, 512, 16)
        DH = D // H
        b, nq, d = Q.shape
        nk = K.shape[1]
        dh = d // H
        q = (Q @ Wq).reshape(b, nq, H, dh).transpose(0, 2, 1, 3)
        k = (K @ Wk).reshape(b, nk, H, dh).transpose(0, 2, 1, 3)
        v = (V @ Wv).reshape(b, nk, H, dh).transpose(0, 2, 1, 3)
        S = jnp.einsum('bhqd,bhkd->bhqk', q, k) / jnp.sqrt(jnp.asarray(dh, (S_dtype := q.dtype)))
        key_pos = jnp.arange(nk)
        mask = key_pos[None, :] < valid_lens[:, None]
        S = jnp.where(mask[:, None, None, :], S, jnp.asarray(-1e+20, S.dtype))
        A = jax.nn.softmax(S, axis=-1)
        O = jnp.einsum('bhqk,bhkd->bhqd', A, v)
        O = O.transpose(0, 2, 1, 3).reshape(b, nq, d)
        return O @ Wo

    def _L0_ffn_ref(hidden_states, gw1, gb1, gw2, gb2, qWm, qU, qS, qV, qb, kWm, kU, kS, kV, kb, vWm, vU, vS, vV, vb, oWm, oU, oS, oV, ob):
        import jax, jax.numpy as jnp
        import numpy as np
        E, TOPK, R = (8, 2, 16)
        D, H, GH = (512, 16, 128)
        HD = D // H
        SCALE = HD ** (-0.5)

        def _svd_moe(x, Wm, U, S, V, b, idx, gates):
            main = jnp.einsum('bsd,od->bso', x, Wm)
            Ug, Sg, Vg = (U[idx], S[idx], V[idx])
            xv = jnp.einsum('bsd,bkrd->bksr', x, Vg)
            xvs = xv * Sg[:, :, None, :]
            eo = jnp.einsum('bksr,bkor->bkso', xvs, Ug)
            expert = jnp.einsum('bkso,bk->bso', eo, gates)
            return main + expert + b
        B, S, _ = hidden_states.shape
        pooled = hidden_states.mean(axis=1)
        h = jax.nn.relu(pooled @ gw1.T + gb1)
        logits = h @ gw2.T + gb2
        top_vals, top_idx = jax.lax.top_k(logits, TOPK)
        gates = jax.nn.softmax(top_vals, axis=-1)
        q = _svd_moe(hidden_states, qWm, qU, qS, qV, qb, top_idx, gates) * SCALE
        k = _svd_moe(hidden_states, kWm, kU, kS, kV, kb, top_idx, gates)
        v = _svd_moe(hidden_states, vWm, vU, vS, vV, vb, top_idx, gates)

        def shp(t):
            return t.reshape(B, S, H, HD).transpose(0, 2, 1, 3)
        q, k, v = (shp(q), shp(k), shp(v))
        attn = jax.nn.softmax(jnp.einsum('bhsd,bhtd->bhst', q, k), axis=-1)
        ctx = jnp.einsum('bhst,bhtd->bhsd', attn, v)
        ctx = ctx.transpose(0, 2, 1, 3).reshape(B, S, D)
        out = _svd_moe(ctx, oWm, oU, oS, oV, ob, top_idx, gates)
        return out
    x = x + _L0_xattn_ref(_layernorm(x, axis=-1), ctx_1024, ctx_1024, _lenS2, L0_xattn_Wq, L0_xattn_Wk, L0_xattn_Wv, L0_xattn_Wo)
    x = x + _L0_ffn_ref(_layernorm(x, axis=-1), L0_ffn_gw1, L0_ffn_gb1, L0_ffn_gw2, L0_ffn_gb2, L0_ffn_qWm, L0_ffn_qU, L0_ffn_qS, L0_ffn_qV, L0_ffn_qb, L0_ffn_kWm, L0_ffn_kU, L0_ffn_kS, L0_ffn_kV, L0_ffn_kb, L0_ffn_vWm, L0_ffn_vU, L0_ffn_vS, L0_ffn_vV, L0_ffn_vb, L0_ffn_oWm, L0_ffn_oU, L0_ffn_oS, L0_ffn_oV, L0_ffn_ob)
    return x

_drawn_inputs = setup_inputs


def setup_inputs(seed=0):
    import zlib

    import numpy as np

    out = dict(_drawn_inputs(seed))
    spreads = {'L0_ffn_gb1': (0.0, 0.8),
     'L0_ffn_gb2': (0.0, 0.8),
     'L0_ffn_qb': (0.0, 0.8),
     'L0_ffn_kb': (0.0, 0.8),
     'L0_ffn_vb': (0.0, 0.1),
     'L0_ffn_ob': (0.0, 0.1)}
    factors = {'L0_ffn_gw1': 8.0,
     'L0_ffn_gw2': 8.0,
     'L0_ffn_qWm': 8.0,
     'L0_ffn_qU': 8.0,
     'L0_ffn_qS': 8.0,
     'L0_ffn_qV': 8.0,
     'L0_ffn_kWm': 8.0,
     'L0_ffn_kU': 8.0,
     'L0_ffn_kS': 8.0,
     'L0_ffn_kV': 8.0,
     'L0_ffn_vU': 8.0,
     'L0_ffn_vS': 8.0,
     'L0_ffn_vV': 8.0,
     'L0_ffn_oU': 8.0,
     'L0_ffn_oS': 8.0,
     'L0_ffn_oV': 8.0}
    for name, (base, spread) in spreads.items():
        noise = np.random.default_rng([zlib.crc32(name.encode()), seed]).standard_normal(out[name].shape)
        drawn = base * np.exp(spread * noise) if base else spread * noise
        out[name] = jnp.asarray(drawn.astype(out[name].dtype))
    for name, factor in factors.items():
        out[name] = (out[name] * factor).astype(out[name].dtype)
    return out
```

```python
from contextlib import ExitStack

import concourse.bass as bass
from concourse import mybir

ALU = mybir.AluOpType
ACT = mybir.ActivationFunctionType
AX = mybir.AxisListType
F32 = mybir.dt.float32
F32R = mybir.dt.float32r
I32 = mybir.dt.int32
U32 = mybir.dt.uint32

P = 128
B, S, D = 8, 512, 512
H, DH = 16, 32
NK = 77
NKP = NK + 1
E, R = 8, 16
DC = D // P
TT = S // P
HJ = H // DC
SCALE = float(DH) ** -0.5
MASKED = -1e20 * float(DH) ** 0.5
EPS = 1e-5
MASK_ROW, SHIFT_ROW = 3 * DH, 3 * DH + 1
ROWS = SHIFT_ROW + 2
QP, KP, VP, OP = range(4)

CROSS, MIX = 0, 1


def attention(half, fill):
    steps = []
    for c in range(DC):
        steps.append(("attend", half, c, *((half, c + 1) if c + 1 < DC else (None, None))))
        if c + 1 < DC:
            steps.append(("shift", half, c + 1))
        if c + 2 < DC:
            steps.append(("proj", half, c + 2))
        steps += fill.get(c, [])
    return steps


def start(half):
    return [("proj", half, 0), ("rowmax", half, 0), ("shift", half, 0), ("proj", half, 1)]


MIX_START = [("weff", QP), ("weff", KP), ("weff", VP), ("vproj",)] + start(MIX)
FINISH_CROSS = [("out1",), ("ln2",)]
GATE = [("xpose",), ("gate_hidden",), ("gate_top",), ("residual",)]
PROLOGUE = ([("load",), ("context",), ("ln1",), ("keys1",), ("xpose",)] + start(CROSS)
            + attention(CROSS, {}) + FINISH_CROSS + GATE)
BODY = (MIX_START
        + [("attend", MIX, 0, MIX, 1), ("shift", MIX, 1), ("proj", MIX, 2), ("load",),
           ("attend", MIX, 1, MIX, 2), ("shift", MIX, 2), ("proj", MIX, 3), ("ln1",), ("keys1",),
           ("attend", MIX, 2, MIX, 3), ("shift", MIX, 3), ("xpose",), ("proj", CROSS, 0),
           ("attend", MIX, 3, CROSS, 0), ("shift", CROSS, 0), ("proj", CROSS, 1)]
        + attention(CROSS, {2: [("weff", OP)]})
        + [("out1",), ("ln2",), ("out2", 0), ("out2", 1), ("xpose",), ("out2", 2),
           ("gate_hidden",), ("out2", 3), ("gate_top",), ("residual",)])
EPILOGUE = MIX_START + attention(MIX, {2: [("weff", OP)]}) + [("out2", t) for t in range(TT)]

BANK_USES = {"context": "D" * (2 * DC + B), "xpose": "A" * TT, "weff": "D" * DC, "vproj": "D" * TT,
             "shift": "D", "out1": "D" * TT, "out2": "D", "gate_hidden": "A", "gate_top": "D"}


def bank_uses(step):
    if step[0] == "proj":
        return "D" if step[1] == CROSS else "DD"
    return BANK_USES.get(step[0], "")


def rowmax_tiles(half):
    return {CROSS: TT, MIX: TT * HJ, None: 0}[half]


def increments(step):
    name, uses = step[0], bank_uses(step)
    n = {"bank_full": len(uses), "act_evacuated": uses.count("A"), "dve_evacuated": uses.count("D")}
    if name == "load":
        n |= {"x_loaded": 16, "v1_loaded": 16}
    if name == "context":
        n |= {"v1_kept": 16 * B}
    if name == "keys1":
        n |= {"keys1_step": 6 + 2 * HJ}
    if name in ("ln1", "ln2"):
        n |= {"ln_step": 2 * TT + 1, "rstd_ready": 1, "xhat_ready": TT}
    if name == "proj":
        n |= {"hi_done": HJ * len(uses), "dup_done": len(uses), "lo_step": HJ * len(uses) - len(uses)}
    if name in ("rowmax", "attend"):
        half = step[1] if name == "rowmax" else step[3]
        n |= {"scores_full": rowmax_tiles(half), "rowmax_done": rowmax_tiles(half)}
    if name == "shift":
        n |= {"shift_hi": 1, "shift_moved": 32}
    if name == "attend":
        keys = S // P if step[1] == MIX else 1
        n |= {"scoresT_full": HJ * keys, "exp_done": HJ * keys, "pv_done": keys,
              "sum_inverted": 1, "normed": 1}
    if name == "weff":
        n |= {f"wm_loaded{dc}": 16 for dc in range(DC)} | {"vs_ready": int(step[1] != OP)}
    if name == "gate_top":
        n |= {"vs_ready": 1, "gate_step": 11, "gate_exp": 1}
    if name == "gate_hidden":
        n |= {"gate_step": 2}
    if name == "residual":
        n |= {"residual_kept": TT}
    if name == "out2":
        n |= {"out_stored": 16}
    return n


def totals(steps):
    n = {}
    for step in steps:
        for key, k in increments(step).items():
            n[key] = n.get(key, 0) + k
    return n


class Count:

    def __init__(self, base, each=None, b=0):
        self.base, self.each, self.b, self.here = base, each or {}, b, {}

    def at(self, name, k=0):
        k += self.here.get(name, 0) + self.base.get(name, 0)
        return self.b * self.each[name] + k if self.each.get(name) else k

    def advance(self, step):
        for name, k in increments(step).items():
            self.here[name] = self.here.get(name, 0) + k


class Banks:

    def __init__(self, before):
        self.last = before
        self.n = 0

    def next(self, engine, at, used):
        waits = []
        if len(self.last) == 2:
            who = self.last[0]
            late = 1 if self.last[1] == who else 0
            names = {"A": ["act_evacuated"], "D": ["dve_evacuated"],
                     "*": ["act_evacuated", "dve_evacuated"]}[who]
            waits = [(name, at(name, 0 if who == "*" else used[who] - late)) for name in names]
        self.last = (self.last + engine)[-2:]
        used[engine] += 1
        self.n += 1
        return (self.n - 1) % 2, waits


def uses_of(steps):
    return "".join(bank_uses(step) for step in steps)


assert len(uses_of(PROLOGUE)) % 2 == 0 and len(uses_of(BODY)) % 2 == 0


def cross_and_mixture_attention(nc, x, ctxT, lens, Wq1, Wk1, Wv1, Wo1, gw1T, gb1, gw2T, gb2,
                                WmT, U, V, SV, qkb, vb, ob, ident, keypos, expert, rowcoef, out, v1_kept_hbm):
    ctx = ExitStack()
    with ctx:
        def sb(name, shape, dt=F32):
            return ctx.enter_context(nc.sbuf_tensor(name, shape, dt))

        def sem(name):
            return ctx.enter_context(nc.semaphore(name))

        Wq1_sb = sb("Wq1_sb", [P, DC, D])
        Wo1_sb = sb("Wo1_sb", [P, DC, D])
        U_sb = sb("U_sb", [P, 4, D])
        V_sb = sb("V_sb", [P, 4, D])
        SV_sb = sb("SV_sb", [P, 4])
        gw1T_sb = sb("gw1T_sb", [P, DC, P])
        gw2T_sb = sb("gw2T_sb", [P, E])
        gb1_sb = sb("gb1_sb", [P, 1])
        gb2_sb = sb("gb2_sb", [P, E])
        qkb_sb = sb("qkb_sb", [P, 2, DC])
        vb_sb = sb("vb_sb", [P, D])
        ob_sb = sb("ob_sb", [P, D])
        ident_sb = sb("ident_sb", [P, P])
        ones = sb("ones", [P, P])
        minus_half = sb("minus_half", [P, TT])
        expert_sb = sb("expert_sb", [P, 1])
        K1T = sb("K1T", [P, DC, B * NK])
        mask_rows = sb("mask_rows", [P, B, NKP])

        x1 = sb("x1", [P, TT, D])
        kept = sb("kept", [P, TT, D])
        xhat = sb("xhat", [P, TT, D])
        XT = sb("XT", [P, DC, S])
        wm_ring = sb("wm_ring", [P, DC, D])
        vs = sb("vs", [P, 2, D])
        Wqk = sb("Wqk", [P, 2, DC, D])
        Wvo = sb("Wvo", [P, DC, D])
        keys1 = sb("keys1", [P, DC, HJ, NKP], F32R)
        k1_hi = sb("k1_hi", [P, DC, NK], F32R)
        k1_lo = sb("k1_lo", [P, DC, NK], F32R)
        V1 = sb("V1", [P, D])
        V2 = sb("V2", [P, TT, D])
        ctx1T = sb("ctx1T", [P, DC, S])
        ctx2T = sb("ctx2T", [P, DC, S])

        qs = sb("qs", [P, 2, HJ, S], F32R)
        ks = sb("ks", [P, 2, HJ, S], F32R)
        probs = sb("probs", [P, 2 * HJ, S])
        inv_sum = sb("inv_sum", [P, S])
        negmax = sb("negmax", [P, P])
        shift = sb("shift", [HJ * TT, 2, P], F32R)

        bn = sb("bn", [P, TT, 6])
        meanvar = sb("meanvar", [P, TT, 2])
        vareps = sb("vareps", [P, TT])
        rstd = sb("rstd", [P, TT])
        pooled = sb("pooled", [P, DC])
        hidden = sb("hidden", [P, 1])
        hiddenB = sb("hiddenB", [P, P])
        logits = sb("logits", [P, E])
        top = sb("top", [P, 8])
        top_at = sb("top_at", [P, 8], U32)
        g = sb("g", [P, 16])
        sel = sb("sel", [P, 2])
        carrier = sb("carrier", [P, 1])
        lens_i = sb("lens_i", [P, B], I32)
        lens_f = sb("lens_f", [P, B])
        keypos_sb = sb("keypos_sb", [P, NKP])
        rowcoef_sb = sb("rowcoef_sb", [P, 2])

        ctxT_sb = probs[:, 0:5, :].rearrange("p a n -> p (a n)")[:, 0:DC * B * NK].rearrange(
            "p (c n) -> p c n", c=DC)
        valid = ks_valid = kept[:, 0:2, :].rearrange("p a n -> p (a n)")[:, 0:B * NKP].rearrange(
            "p (b n) -> p b n", b=B)
        Wk1_sb, Wv1_sb = Wqk[:, 1], Wvo

        def bank(name, n):
            return ctx.enter_context(nc.psum_tensor(name, [P, n, 512], F32))

        pj = bank("pj", 2)
        sc = bank("sc", 2)
        scT = bank("scT", 2)
        acc = bank("acc", 1)
        den = bank("den", 1)

        names = sorted({k for s in (PROLOGUE, BODY, EPILOGUE) for k in totals(s)})
        sems = {name: sem(name) for name in names}
        weights_loaded = sem("weights_loaded")
        context_loaded = sem("context_loaded")
        consts_loaded = sem("consts_loaded")
        consts_made = sem("consts_made")
        mask_step = sem("mask_step")

        def walk(engine, loop, handlers):
            pro, each = totals(PROLOGUE), totals(BODY)

            def segment(steps, count, before):
                banks = Banks(before)
                for step in steps:
                    if step[0] in handlers:
                        handlers[step[0]](count, step, banks)
                    elif bank_uses(step):
                        banks.last = (banks.last + bank_uses(step))[-2:]
                        banks.n += len(bank_uses(step))
                    count.advance(step)

            def row(n):
                return n

            c = Count({})
            c.row, c.ahead = None, row(0)
            segment(PROLOGUE, c, "")
            with loop(0, B - 1) as b:
                c = Count(pro, each, b)
                c.row, c.ahead = b, b + 1
                segment(BODY, c, "**")
            c = Count({k: pro.get(k, 0) + (B - 1) * each.get(k, 0) for k in {**pro, **each}})
            c.row, c.ahead = B - 1, None
            segment(EPILOGUE, c, "**")

        def rows(start, n):
            return slice(start, start + n) if isinstance(start, int) else bass.ds(start, n)

        block = ctx.enter_context(nc.Block())

        @block.sync
        def _(sp):
            for dst, src in ((ctxT_sb, ctxT.rearrange("(c p) n -> p c n", p=P)),
                             (Wk1_sb, Wk1.rearrange("(c p) n -> p c n", p=P))):
                sp.dma_start(dst, src).then_inc(context_loaded, 16)
            for dst, src in ((keypos_sb[:], keypos), (lens_i[:], lens.rearrange("(a n) -> a n", a=1)
                                                      .to_broadcast([P, B])),
                             (rowcoef_sb[:], rowcoef), (ident_sb[:], ident)):
                sp.dma_start(dst, src).then_inc(consts_loaded, 16)
            sp.dma_start(Wv1_sb[:], Wv1.rearrange("(c p) n -> p c n", p=P)).then_inc(context_loaded, 16)

            def load(c, step, banks):
                if c.row is not None:
                    sp.wait_ge(sems["residual_kept"], c.at("residual_kept"))
                    sp.wait_ge(sems["pv_done"], c.at("pv_done"))
                sp.dma_start(x1[:], x[rows(c.ahead, 1)].rearrange("a (t p) d -> p (a t) d", p=P))\
                  .then_inc(sems["x_loaded"], 16)
                if c.row is not None:
                    sp.dma_start(V1[0:NK, :], v1_kept_hbm[rows(c.ahead, 1)].rearrange("a k d -> k (a d)"))\
                      .then_inc(sems["v1_loaded"], 16)

            def context(c, step, banks):
                for dst, src in ((Wq1_sb[:], Wq1.rearrange("(c p) n -> p c n", p=P)),
                                 (Wo1_sb[:], Wo1.rearrange("(c p) n -> p c n", p=P)),
                                 (U_sb[:], U), (V_sb[:], V), (SV_sb[:], SV),
                                 (gw1T_sb[:], gw1T.rearrange("(c p) n -> p c n", p=P)),
                                 (gw2T_sb[:], gw2T), (gb1_sb[:], gb1.rearrange("(p a) -> p a", a=1)),
                                 (gb2_sb[:], gb2.rearrange("(a n) -> a n", a=1).to_broadcast([P, E])),
                                 (qkb_sb[:], qkb),
                                 (vb_sb[:], vb.rearrange("(a n) -> a n", a=1).to_broadcast([P, D])),
                                 (ob_sb[:], ob.rearrange("(a n) -> a n", a=1).to_broadcast([P, D])),
                                 (expert_sb[:], expert)):
                    sp.dma_start(dst, src).then_inc(weights_loaded, 16)
                for dc in range(DC):
                    sp.dma_start(wm_ring[:, dc, :], WmT[QP, dc * P:(dc + 1) * P, :])\
                      .then_inc(sems[f"wm_loaded{dc}"], 16)
                for b in range(B):
                    sp.wait_ge(sems["dve_evacuated"], c.at("dve_evacuated", 2 * DC + b + 1))
                    sp.dma_start(v1_kept_hbm[b], xhat[0:NK, b % TT, :]).then_inc(sems["v1_kept"], 16)
                sp.wait_ge(sems["v1_kept"], 16 * B)
                sp.dma_start(V1[0:NK, :], v1_kept_hbm[0]).then_inc(sems["v1_loaded"], 16)

            def weff(c, step, banks):
                nxt = (step[1] + 1) % 4
                if step[1] == OP and c.ahead is None:
                    return
                for dc in range(DC):
                    sp.wait_ge(sems["dve_evacuated"], c.at("dve_evacuated", dc + 1))
                    sp.dma_start(wm_ring[:, dc, :], WmT[nxt, dc * P:(dc + 1) * P, :])\
                      .then_inc(sems[f"wm_loaded{dc}"], 16)

            def move_shift(c, step, banks):
                sp.wait_ge(sems["dve_evacuated"], c.at("dve_evacuated", 1))
                for part in range(2):
                    row = SHIFT_ROW + part
                    sp.dma_start(qs[row:row + 1, step[2] % 2, :, :].rearrange("p j (t n) -> p (j t) n", n=P)
                                 .bitcast(F32), shift[:, part, :].bitcast(F32))\
                      .then_inc(sems["shift_moved"], 16)

            def out2(c, step, banks):
                t = step[1]
                sp.wait_ge(sems["dve_evacuated"], c.at("dve_evacuated", 1))
                sp.dma_start(out[rows(c.row, 1), t * P:(t + 1) * P, :].rearrange("a p d -> p (a d)"),
                             kept[:, t, :]).then_inc(sems["out_stored"], 16)

            walk(sp, sp.Fori, {"load": load, "context": context, "weff": weff, "shift": move_shift,
                               "out2": out2})
            sp.wait_ge(sems["out_stored"], 16 * B * TT)

        @block.gpsimd
        def _(pool):
            for n, (what, value) in enumerate((
                    (ones[:], 1.0), (minus_half[:], -0.5), (negmax[:], 0.0),
                    (qs[MASK_ROW:MASK_ROW + 1, :, :, :].bitcast(F32), 1.0),
                    (ks[MASK_ROW:ROWS, :, :, :].bitcast(F32), 1.0),
                    (ks[MASK_ROW:MASK_ROW + 1, :, :, :].bitcast(F32), 0.0))):
                nc.gpsimd.memset(what, value).then_inc(consts_made, 1)
                pool.wait_ge(consts_made, n + 1)

            def inverse_deviation(c, step, banks):
                pool.wait_ge(sems["ln_step"], c.at("ln_step", 2 * TT + 1))
                if c.row is not None or step[0] == "ln2":
                    pool.wait_ge(sems["xhat_ready"], c.at("xhat_ready"))
                nc.gpsimd.tensor_tensor(rstd[:], vareps[:], minus_half[:], ALU.pow)\
                    .then_inc(sems["rstd_ready"], 1)

            def residual(c, step, banks):
                pool.wait_ge(sems["dve_evacuated"], c.at("dve_evacuated"))
                if c.row is None:
                    pool.wait_ge(weights_loaded, 16 * 13)
                else:
                    pool.wait_ge(sems["out_stored"], c.at("out_stored"))
                for t in range(TT):
                    nc.gpsimd.tensor_tensor(kept[:, t, :], x1[:, t, :], ob_sb[:], ALU.add)\
                        .then_inc(sems["residual_kept"], 1)

            walk(pool, pool.Fori, {"ln1": inverse_deviation, "ln2": inverse_deviation,
                                   "residual": residual})

        @block.scalar
        def _(act):
            def xpose(c, step, banks):
                for t in range(TT):
                    p, _ = banks.next("A", c.at, {"A": 0, "D": 0})
                    act.wait_ge(sems["bank_full"], c.at("bank_full", t + 1))
                    nc.scalar.activation(XT[:, :, t * P:(t + 1) * P],
                                         pj[:, p, :].rearrange("p (c n) -> p c n", c=DC),
                                         ACT.Copy).then_inc(sems["act_evacuated"], 1)

            def proj(c, step, banks):
                _, half, job = step
                slot = job % 2
                for w, stack in ((0, qs), (1, ks))[:len(bank_uses(step))]:
                    p, _ = banks.next("D", c.at, {"A": 0, "D": 0})
                    act.wait_ge(sems["bank_full"], c.at("bank_full", w + 1))
                    for j in range(HJ):
                        src = pj[j * DH:(j + 1) * DH, p, :]
                        dst = stack[0:DH, slot, j, :]
                        if half == MIX:
                            ins = nc.scalar.activation(dst, src, ACT.Identity,
                                                       bias=qkb_sb[j * DH:(j + 1) * DH, w, job:job + 1])
                        else:
                            ins = nc.scalar.activation(dst, src, ACT.Copy)
                        ins.then_inc(sems["hi_done"], 1)
                    act.wait_ge(sems["hi_done"], c.at("hi_done", (w + 1) * HJ))
                    at = (DH, 2 * DH)[w]
                    nc.scalar.activation(stack[at:at + DH, slot, :, :],
                                         stack[0:DH, slot, :, :].bitcast(F32), ACT.Copy)\
                        .then_inc(sems["dup_done"], 1)

            def attend(c, step, banks):
                _, half, job, *_ = step
                key_tiles = TT if half == MIX else 1
                keys = P if half == MIX else NK
                for kt in range(key_tiles):
                    side = (kt if half == MIX else job) % 2
                    first = c.row is None and job + kt < 2
                    if not first:
                        act.wait_ge(sems["pv_done"], c.at("pv_done", kt - 1))
                    for j in range(HJ):
                        n = kt * HJ + j
                        act.wait_ge(sems["scoresT_full"], c.at("scoresT_full", n + 1))
                        nc.scalar.activation(probs[0:keys, side * HJ + j, :], scT[0:keys, n % 2, :],
                                             ACT.Exp, scale=SCALE).then_inc(sems["exp_done"], 1)

            def gate_hidden(c, step, banks):
                p, _ = banks.next("A", c.at, {"A": 0, "D": 0})
                if c.row is None:
                    act.wait_ge(weights_loaded, 16 * 13)
                act.wait_ge(sems["bank_full"], c.at("bank_full", 1))
                nc.scalar.activation(hidden[:], pj[:, p, 0:1], ACT.Relu, bias=gb1_sb[:], scale=1.0 / S)\
                    .then_inc(sems["act_evacuated"], 1)

            def gate_top(c, step, banks):
                act.wait_ge(sems["gate_step"], c.at("gate_step", 4))
                nc.scalar.activation(g[:, 1:2], g[:, 0:1], ACT.Exp).then_inc(sems["gate_exp"], 1)

            walk(act, act.Fori, {"xpose": xpose, "proj": proj, "attend": attend,
                                 "gate_hidden": gate_hidden, "gate_top": gate_top})

        @block.vector
        def _(dve):
            def settle(semaphore, value):
                dve.wait_ge(semaphore, value)
                nc.vector.memset(carrier[:], 0.0)

            dve.wait_ge(consts_loaded, 64)
            nc.vector.tensor_copy(lens_f[:], lens_i[:]).then_inc(mask_step, 1)
            dve.wait_ge(mask_step, 1)
            for b in range(B):
                nc.vector.tensor_scalar(valid[:, b, :], keypos_sb[:], lens_f[:, b:b + 1], None, ALU.is_lt)\
                    .then_inc(mask_step, 1)
            dve.wait_ge(mask_step, B + 1)
            nc.vector.tensor_scalar(mask_rows[MASK_ROW:ROWS, :, :], valid[MASK_ROW:ROWS, :, :],
                                    rowcoef_sb[MASK_ROW:ROWS, 0:1], rowcoef_sb[MASK_ROW:ROWS, 1:2],
                                    ALU.mult, ALU.add).then_inc(mask_step, 1)
            dve.wait_ge(mask_step, B + 2)

            def context(c, step, banks):
                n = 0
                for co in range(DC):
                    for half in range(2):
                        p, _ = banks.next("D", c.at, {"A": 0, "D": 0})
                        n += 1
                        dve.wait_ge(sems["bank_full"], n)
                        nc.vector.tensor_tensor(
                            K1T[:, co, half * 4 * NK:(half + 1) * 4 * NK].rearrange("p (b k) -> p b k", k=NK),
                            pj[:, p, 0:4 * NK].rearrange("p (b k) -> p b k", k=NK),
                            valid[:, 4 * half:4 * half + 4, 0:NK], ALU.mult)\
                            .then_inc(sems["dve_evacuated"], 1)
                for b in range(B):
                    p, _ = banks.next("D", c.at, {"A": 0, "D": 0})
                    n += 1
                    dve.wait_ge(sems["bank_full"], n)
                    if b >= TT:
                        dve.wait_ge(sems["v1_kept"], 16 * TT)
                    nc.vector.tensor_copy(xhat[0:NK, b % TT, :], pj[0:NK, p, :])\
                        .then_inc(sems["dve_evacuated"], 1)

            def keys1_stack(c, step, banks):
                done = 0

                def then(ins):
                    nonlocal done
                    done += 1
                    ins.then_inc(sems["keys1_step"], 1)

                if c.row is None:
                    dve.wait_ge(sems["dve_evacuated"], c.at("dve_evacuated"))
                else:
                    dve.wait_ge(sems["pv_done"], c.at("pv_done", -1))
                src = K1T[:, :, rows(c.ahead * NK, NK)]
                then(nc.vector.tensor_copy(k1_hi[:], src))
                then(nc.vector.tensor_copy(keys1[MASK_ROW:ROWS, :, :, :].rearrange("p c j k -> p (c j) k"),
                                           mask_rows[MASK_ROW:ROWS, rows(c.ahead, 1), :]
                                           .to_broadcast([ROWS - MASK_ROW, H, NKP])))
                dve.wait_ge(sems["keys1_step"], c.at("keys1_step", done))
                then(nc.vector.tensor_tensor(k1_lo[:], src, k1_hi[:].bitcast(F32), ALU.subtract))
                if c.row is None:
                    nc.vector.memset(keys1[0:3 * DH, :, :, NK:NKP].bitcast(F32), 0.0).then_inc(mask_step, 1)
                for j in range(HJ):
                    then(nc.vector.tensor_copy(keys1[0:DH, :, j, 0:NK],
                                               k1_hi[j * DH:(j + 1) * DH].bitcast(F32)))
                dve.wait_ge(sems["keys1_step"], c.at("keys1_step", done))
                for j in range(HJ):
                    then(nc.vector.tensor_copy(keys1[DH:2 * DH, :, j, 0:NK],
                                               k1_lo[j * DH:(j + 1) * DH].bitcast(F32)))
                for half in range(3):
                    a, b = ((0, 2), (2, 3), (3, 4))[half]
                    then(nc.vector.tensor_copy(keys1[2 * DH:3 * DH, a:b, :, 0:NK],
                                               keys1[0:DH, a:b, :, 0:NK].bitcast(F32)))

            def layernorm(c, step, banks):
                for t in range(TT):
                    if step[0] == "ln1":
                        if t == 0:
                            dve.wait_ge(sems["x_loaded"], c.at("x_loaded"))
                    else:
                        dve.wait_ge(sems["dve_evacuated"], c.at("dve_evacuated", t + 1 - TT))
                    nc.vector.bn_stats(bn[:, t, :], x1[:, t, :]).then_inc(sems["ln_step"], 1)
                settle(sems["ln_step"], c.at("ln_step", TT))
                for t in range(TT):
                    nc.vector.bn_aggr(meanvar[:, t, :], bn[:, t, :]).then_inc(sems["ln_step"], 1)
                dve.wait_ge(sems["ln_step"], c.at("ln_step", 2 * TT))
                nc.vector.tensor_scalar(vareps[:], meanvar[:, :, 1], EPS, None, ALU.add)\
                    .then_inc(sems["ln_step"], 1)
                dve.wait_ge(sems["rstd_ready"], c.at("rstd_ready", 1))
                dve.wait_ge(sems["bank_full"], c.at("bank_full"))
                if c.row is None and step[0] == "ln1":
                    dve.wait_ge(sems["v1_kept"], 16 * B)
                for t in range(TT):
                    nc.vector.tensor_scalar(xhat[:, t, :], x1[:, t, :], meanvar[:, t, 0:1], rstd[:, t:t + 1],
                                            ALU.subtract, ALU.mult).then_inc(sems["xhat_ready"], 1)

            def proj(c, step, banks):
                _, half, job = step
                slot = job % 2
                for w, stack in ((0, qs), (1, ks))[:len(bank_uses(step))]:
                    p, _ = banks.next("D", c.at, {"A": 0, "D": 0})
                    at = (2 * DH, DH)[w]
                    for j in range(HJ):
                        dve.wait_ge(sems["hi_done"], c.at("hi_done", w * HJ + j + 1))
                        src = pj[j * DH:(j + 1) * DH, p, :]
                        bias = qkb_sb[j * DH:(j + 1) * DH, w, job:job + 1] if half == MIX else 0.0
                        nc.vector.scalar_tensor_tensor(stack[at:at + DH, slot, j, :], src, bias,
                                                       stack[0:DH, slot, j, :].bitcast(F32),
                                                       ALU.add, ALU.subtract)\
                            .then_inc(sems["dve_evacuated" if j == HJ - 1 else "lo_step"], 1)

            def reduce_scores(c, half, n):
                dve.wait_ge(sems["scores_full"], c.at("scores_full", n + 1))
                if half == MIX:
                    nc.vector.tensor_reduce(negmax[:, n:n + 1], sc[:, n % 2, :], AX.X, ALU.max, negate=True)\
                        .then_inc(sems["rowmax_done"], 1)
                else:
                    nc.vector.tensor_reduce(negmax[:, n:HJ * TT:TT],
                                            sc[:, n % 2, 0:HJ * NKP].rearrange("p (j k) -> p j k", j=HJ),
                                            AX.X, ALU.max, negate=True).then_inc(sems["rowmax_done"], 1)

            def rowmax(c, step, banks):
                if c.row is None:
                    dve.wait_ge(consts_made, 6)
                for n in range(rowmax_tiles(step[1])):
                    reduce_scores(c, step[1], n)

            def shift_parts(c, step, banks):
                p, _ = banks.next("D", c.at, {"A": 0, "D": 0})
                dve.wait_ge(sems["bank_full"], c.at("bank_full", 1))
                if c.at("shift_moved") is not 0:
                    dve.wait_ge(sems["shift_moved"], c.at("shift_moved"))
                nc.vector.tensor_copy(shift[:, 0, :], pj[0:HJ * TT, p, 0:P]).then_inc(sems["shift_hi"], 1)
                dve.wait_ge(sems["shift_hi"], c.at("shift_hi", 1))
                nc.vector.tensor_tensor(shift[:, 1, :], pj[0:HJ * TT, p, 0:P], shift[:, 0, :].bitcast(F32),
                                        ALU.subtract).then_inc(sems["dve_evacuated"], 1)

            def attend(c, step, banks):
                _, half, job, nxt, _ = step
                for n in range(rowmax_tiles(nxt)):
                    reduce_scores(c, nxt, n)
                dve.wait_ge(sems["pv_done"], c.at("pv_done", TT if half == MIX else 1))
                if c.at("normed") is not 0:
                    dve.wait_ge(sems["normed"], c.at("normed"))
                nc.vector.reciprocal(inv_sum[:], den[:, 0, :]).then_inc(sems["sum_inverted"], 1)
                dve.wait_ge(sems["sum_inverted"], c.at("sum_inverted", 1))
                dst = (ctx1T, ctx2T)[half]
                nc.vector.tensor_tensor(dst[:, job, :], acc[:, 0, :], inv_sum[:], ALU.mult)\
                    .then_inc(sems["normed"], 1)

            def scale_v(c, p, k):
                dve.wait_ge(sems["bank_full"], c.at("bank_full", k))
                nc.vector.tensor_scalar(vs[:, p % 2, :], V_sb[:, p, :], g[:, 10 + p:11 + p], None, ALU.mult)\
                    .then_inc(sems["vs_ready"], 1)

            def weff(c, step, banks):
                p = step[1]
                if p != OP:
                    scale_v(c, p + 1, 0)
                dst = Wvo if p in (VP, OP) else Wqk[:, p]
                for dc in range(DC):
                    b, _ = banks.next("D", c.at, {"A": 0, "D": 0})
                    dve.wait_ge(sems[f"wm_loaded{dc}"], c.at(f"wm_loaded{dc}", 16))
                    dve.wait_ge(sems["bank_full"], c.at("bank_full", dc + 1))
                    nc.vector.tensor_tensor(dst[:, dc, :], pj[:, b, :], wm_ring[:, dc, :], ALU.add)\
                        .then_inc(sems["dve_evacuated"], 1)

            def vproj(c, step, banks):
                for t in range(TT):
                    p, _ = banks.next("D", c.at, {"A": 0, "D": 0})
                    dve.wait_ge(sems["bank_full"], c.at("bank_full", t + 1))
                    nc.vector.tensor_tensor(V2[:, t, :], pj[:, p, :], vb_sb[:], ALU.add)\
                        .then_inc(sems["dve_evacuated"], 1)

            def out1(c, step, banks):
                for t in range(TT):
                    p, _ = banks.next("D", c.at, {"A": 0, "D": 0})
                    dve.wait_ge(sems["bank_full"], c.at("bank_full", t + 1))
                    nc.vector.tensor_tensor(x1[:, t, :], pj[:, p, :], x1[:, t, :], ALU.add)\
                        .then_inc(sems["dve_evacuated"], 1)

            def out2(c, step, banks):
                t = step[1]
                p, _ = banks.next("D", c.at, {"A": 0, "D": 0})
                dve.wait_ge(sems["residual_kept"], c.at("residual_kept"))
                dve.wait_ge(sems["bank_full"], c.at("bank_full", 1))
                nc.vector.tensor_tensor(kept[:, t, :], pj[:, p, :], kept[:, t, :], ALU.add)\
                    .then_inc(sems["dve_evacuated"], 1)

            def gate_hidden(c, step, banks):
                banks.next("A", c.at, {"A": 0, "D": 0})
                dve.wait_ge(sems["act_evacuated"], c.at("act_evacuated"))
                nc.vector.tensor_reduce(pooled[:], XT[:], AX.X, ALU.add).then_inc(sems["gate_step"], 1)
                dve.wait_ge(sems["act_evacuated"], c.at("act_evacuated", 1))
                nc.vector.tensor_scalar(hiddenB[:], ones[:], hidden[:, 0:1], None, ALU.mult)\
                    .then_inc(sems["gate_step"], 1)

            def gate_top(c, step, banks):
                p, _ = banks.next("D", c.at, {"A": 0, "D": 0})
                n = 0

                def step_done(ins):
                    nonlocal n
                    n += 1
                    ins.then_inc(sems["gate_step"], 1)
                    wait = settle if n == 1 else dve.wait_ge
                    wait(sems["gate_step"], c.at("gate_step", n))

                dve.wait_ge(sems["bank_full"], c.at("bank_full", 1))
                nc.vector.tensor_tensor(logits[:], pj[:, p, 0:E], gb2_sb[:], ALU.add)\
                    .then_inc(sems["dve_evacuated"], 1)
                settle(sems["dve_evacuated"], c.at("dve_evacuated", 1))
                step_done(nc.vector.max(top[:], logits[:]))
                step_done(nc.vector.max_index(top_at[:], top[:], logits[:]))
                step_done(nc.vector.tensor_copy(g[:, 2:4], top_at[:, 0:2]))
                step_done(nc.vector.tensor_tensor(g[:, 0:1], top[:, 1:2], top[:, 0:1], ALU.subtract))
                dve.wait_ge(sems["gate_exp"], c.at("gate_exp", 1))
                step_done(nc.vector.tensor_scalar(g[:, 4:5], g[:, 1:2], 1.0, None, ALU.add))
                step_done(nc.vector.reciprocal(g[:, 5:6], g[:, 4:5]))
                step_done(nc.vector.tensor_tensor(g[:, 6:7], g[:, 5:6], g[:, 1:2], ALU.mult))
                step_done(nc.vector.tensor_scalar(sel[:], g[:, 2:4], expert_sb[:, 0:1], None, ALU.is_equal))
                step_done(nc.vector.tensor_tensor(g[:, 7:9], sel[:], g[:, 5:7], ALU.mult))
                step_done(nc.vector.tensor_tensor(g[:, 9:10], g[:, 7:8], g[:, 8:9], ALU.add))
                step_done(nc.vector.tensor_scalar(g[:, 10:14], SV_sb[:], g[:, 9:10], None, ALU.mult))
                scale_v(c, QP, 0)

            walk(dve, dve.Fori, {"context": context, "keys1": keys1_stack, "ln1": layernorm,
                                 "ln2": layernorm, "proj": proj, "rowmax": rowmax, "shift": shift_parts,
                                 "attend": attend, "weff": weff, "vproj": vproj, "out1": out1,
                                 "out2": out2, "gate_hidden": gate_hidden, "gate_top": gate_top})

        @block.tensor
        def _(pe):
            pe.wait_ge(consts_loaded, 64)
            pe.wait_ge(consts_made, 6)

            def take(c, banks, engine, used):
                p, waits = banks.next(engine, c.at, used)
                for name, value in waits:
                    pe.wait_ge(sems[name], value)
                return p

            def context(c, step, banks):
                used = {"A": 0, "D": 0}
                pe.wait_ge(context_loaded, 48)
                for co in range(DC):
                    for half in range(2):
                        p = take(c, banks, "D", used)
                        for dc in range(DC):
                            mm = nc.tensor.matmul(pj[:, p, 0:4 * NK], Wk1_sb[:, dc, co * P:(co + 1) * P],
                                                  ctxT_sb[:, dc, half * 4 * NK:(half + 1) * 4 * NK],
                                                  start=(dc == 0), stop=(dc == DC - 1))
                        mm.then_inc(sems["bank_full"], 1)
                for b in range(B):
                    p = take(c, banks, "D", used)
                    for dc in range(DC):
                        mm = nc.tensor.matmul(pj[0:NK, p, :], ctxT_sb[:, dc, b * NK:(b + 1) * NK],
                                              Wv1_sb[:, dc, :], start=(dc == 0), stop=(dc == DC - 1))
                    mm.then_inc(sems["bank_full"], 1)

            def xpose(c, step, banks):
                used = {"A": 0, "D": 0}
                for t in range(TT):
                    p = take(c, banks, "A", used)
                    pe.wait_ge(sems["xhat_ready"], c.at("xhat_ready", t + 1 - TT))
                    for dc in range(DC):
                        mm = nc.tensor.transpose(pj[:, p, dc * P:(dc + 1) * P], xhat[:, t, dc * P:(dc + 1) * P],
                                                 ident_sb[:])
                    mm.then_inc(sems["bank_full"], 1)

            def proj(c, step, banks):
                _, half, job = step
                used = {"A": 0, "D": 0}
                if c.row is None:
                    pe.wait_ge(weights_loaded, 16 * 13)
                pe.wait_ge(sems["act_evacuated"], c.at("act_evacuated"))
                if half == MIX:
                    pe.wait_ge(sems["dve_evacuated"], c.at("dve_evacuated"))
                for w in range(len(bank_uses(step))):
                    p = take(c, banks, "D", used)
                    W = Wq1_sb if half == CROSS else Wqk[:, w]
                    for dc in range(DC):
                        mm = nc.tensor.matmul(pj[:, p, :], W[:, dc, job * P:(job + 1) * P], XT[:, dc, :],
                                              start=(dc == 0), stop=(dc == DC - 1))
                    mm.then_inc(sems["bank_full"], 1)

            def score_tile(c, half, job, n):
                slot = job % 2
                if n >= 2:
                    pe.wait_ge(sems["rowmax_done"], c.at("rowmax_done", n - 1))
                if half == MIX:
                    j, t = n // TT, n % TT
                    nc.tensor.matmul(sc[:, n % 2, :], qs[0:3 * DH, slot, j, t * P:(t + 1) * P],
                                     ks[0:3 * DH, slot, j, :], start=True, stop=True)\
                        .then_inc(sems["scores_full"], 1)
                else:
                    for j in range(HJ):
                        mm = nc.tensor.matmul(sc[:, n % 2, j * NKP:(j + 1) * NKP],
                                              qs[0:MASK_ROW + 1, slot, j, n * P:(n + 1) * P],
                                              keys1[0:MASK_ROW + 1, job, j, :], start=True, stop=True)
                    mm.then_inc(sems["scores_full"], 1)

            def stacks_ready(c, half):
                pe.wait_ge(sems["dve_evacuated"], c.at("dve_evacuated"))
                pe.wait_ge(sems["dup_done"], c.at("dup_done"))
                if half == CROSS:
                    pe.wait_ge(sems["keys1_step"], c.at("keys1_step"))
                if c.at("rowmax_done") is not 0:
                    pe.wait_ge(sems["rowmax_done"], c.at("rowmax_done"))

            def rowmax(c, step, banks):
                _, half, job = step
                if c.row is None:
                    pe.wait_ge(mask_step, B + 3)
                stacks_ready(c, half)
                for n in range(rowmax_tiles(half)):
                    score_tile(c, half, job, n)

            def turn_shift(c, step, banks):
                p = take(c, banks, "D", {"A": 0, "D": 0})
                pe.wait_ge(sems["rowmax_done"], c.at("rowmax_done"))
                nc.tensor.transpose(pj[:, p, 0:P], negmax[:], ident_sb[:]).then_inc(sems["bank_full"], 1)

            def attend(c, step, banks):
                _, half, job, nxt, nxt_job = step
                slot = job % 2
                key_tiles = TT if half == MIX else 1
                keys = P if half == MIX else NK
                todo = list(range(rowmax_tiles(nxt)))
                pe.wait_ge(sems["shift_moved"], c.at("shift_moved"))
                if half == CROSS:
                    pe.wait_ge(sems["v1_loaded"], c.at("v1_loaded"))
                if nxt is not None:
                    stacks_ready(c, nxt)

                def scores_transposed(kt, j):
                    n = kt * HJ + j
                    if not (c.row is None and job == 0 and n < 2):
                        pe.wait_ge(sems["exp_done"], c.at("exp_done", n - 1))
                    lhsT = (ks[0:ROWS, slot, j, kt * P:(kt + 1) * P] if half == MIX
                            else keys1[0:ROWS, job, j, 0:NK])
                    nc.tensor.matmul(scT[0:keys, n % 2, :], lhsT, qs[0:ROWS, slot, j, :],
                                     start=True, stop=True).then_inc(sems["scoresT_full"], 1)

                def fill(k):
                    for _ in range(k):
                        if todo:
                            score_tile(c, nxt, nxt_job, todo.pop(0))

                def p_times_v(kt):
                    side = (kt if half == MIX else job) % 2
                    pe.wait_ge(sems["exp_done"], c.at("exp_done", HJ * (kt + 1)))
                    if kt == 0 and not (c.row is None and job == 0):
                        pe.wait_ge(sems["normed"], c.at("normed"))
                    for to in (acc, den):
                        for j in range(HJ):
                            head = (job * HJ + j) * DH
                            lhsT = (ones[0:keys, 0:DH] if to is den else
                                    V2[:, kt, head:head + DH] if half == MIX else V1[0:NK, head:head + DH])
                            mm = nc.tensor.matmul(to[j * DH:(j + 1) * DH, 0, :], lhsT,
                                                  probs[0:keys, side * HJ + j, :],
                                                  start=(kt == 0), stop=(kt == key_tiles - 1))
                    mm.then_inc(sems["pv_done"], 1)

                each = -(-len(todo) // key_tiles // 2)
                for kt in range(key_tiles + 1):
                    if kt < key_tiles:
                        for j in range(HJ):
                            scores_transposed(kt, j)
                            if j % 2 and kt:
                                fill(each)
                    if kt:
                        if kt == key_tiles:
                            fill(len(todo))
                        p_times_v(kt - 1)

            def weff(c, step, banks):
                p = step[1]
                used = {"A": 0, "D": 0}
                pe.wait_ge(sems["vs_ready"], c.at("vs_ready"))
                for dc in range(DC):
                    b = take(c, banks, "D", used)
                    nc.tensor.matmul(pj[:, b, :], vs[:, p % 2, dc * P:(dc + 1) * P], U_sb[:, p, :],
                                     start=True, stop=True).then_inc(sems["bank_full"], 1)

            def vproj(c, step, banks):
                used = {"A": 0, "D": 0}
                pe.wait_ge(sems["act_evacuated"], c.at("act_evacuated"))
                pe.wait_ge(sems["dve_evacuated"], c.at("dve_evacuated"))
                for t in range(TT):
                    p = take(c, banks, "D", used)
                    for dc in range(DC):
                        mm = nc.tensor.matmul(pj[:, p, :], XT[:, dc, t * P:(t + 1) * P], Wvo[:, dc, :],
                                              start=(dc == 0), stop=(dc == DC - 1))
                    mm.then_inc(sems["bank_full"], 1)

            def project_out(c, banks, used, srcT, W, t):
                p = take(c, banks, "D", used)
                for dc in range(DC):
                    mm = nc.tensor.matmul(pj[:, p, :], srcT[:, dc, t * P:(t + 1) * P], W[:, dc, :],
                                          start=(dc == 0), stop=(dc == DC - 1))
                mm.then_inc(sems["bank_full"], 1)

            def out1(c, step, banks):
                used = {"A": 0, "D": 0}
                pe.wait_ge(sems["normed"], c.at("normed"))
                for t in range(TT):
                    project_out(c, banks, used, ctx1T, Wo1_sb, t)

            def out2(c, step, banks):
                pe.wait_ge(sems["normed"], c.at("normed"))
                pe.wait_ge(sems["dve_evacuated"], c.at("dve_evacuated"))
                project_out(c, banks, {"A": 0, "D": 0}, ctx2T, Wvo, step[1])

            def gate_hidden(c, step, banks):
                p = take(c, banks, "A", {"A": 0, "D": 0})
                pe.wait_ge(sems["gate_step"], c.at("gate_step", 1))
                for dc in range(DC):
                    mm = nc.tensor.matmul(pj[:, p, 0:1], gw1T_sb[:, dc, :], pooled[:, dc:dc + 1],
                                          start=(dc == 0), stop=(dc == DC - 1))
                mm.then_inc(sems["bank_full"], 1)

            def gate_top(c, step, banks):
                p = take(c, banks, "D", {"A": 0, "D": 0})
                pe.wait_ge(sems["gate_step"], c.at("gate_step"))
                nc.tensor.matmul(pj[:, p, 0:E], hiddenB[:], gw2T_sb[:], start=True, stop=True)\
                    .then_inc(sems["bank_full"], 1)

            walk(pe, pe.Fori, {"context": context, "xpose": xpose, "proj": proj, "rowmax": rowmax,
                               "shift": turn_shift, "attend": attend, "weff": weff, "vproj": vproj,
                               "out1": out1, "out2": out2, "gate_hidden": gate_hidden,
                               "gate_top": gate_top})


def kernel(x, ctx_1024, _lenS2, L0_xattn_Wq, L0_xattn_Wk, L0_xattn_Wv, L0_xattn_Wo, **ffn):
    import numpy as np
    import concourse.bacc as bacc
    from concourse.bass_utils import run_bass_kernel_spmd

    w = {k.removeprefix("L0_ffn_"): np.asarray(v) for k, v in ffn.items()}
    at = np.arange(P)
    rowcoef = np.zeros((P, 2), np.float32)
    rowcoef[MASK_ROW] = (-MASKED, MASKED)
    rowcoef[SHIFT_ROW:ROWS] = (0.0, 1.0)
    keypos = np.full((P, NKP), 1e9, np.float32)
    keypos[:, :NK] = np.arange(NK)
    ins = {
        "x": x,
        "ctxT": np.asarray(ctx_1024).reshape(B * NK, D).T,
        "lens": np.asarray(_lenS2),
        "Wq1": L0_xattn_Wq, "Wk1": L0_xattn_Wk, "Wv1": L0_xattn_Wv, "Wo1": L0_xattn_Wo,
        "gw1T": w["gw1"].T, "gb1": w["gb1"], "gw2T": w["gw2"].T, "gb2": w["gb2"],
        "WmT": np.stack([w[p + "Wm"].T for p in "qkvo"]),
        "U": np.stack([w[p + "U"].transpose(0, 2, 1).reshape(E * R, D) for p in "qkvo"], 1),
        "V": np.stack([w[p + "V"].reshape(E * R, D) for p in "qkvo"], 1),
        "SV": np.stack([w[p + "S"].reshape(E * R) for p in "qkvo"], 1),
        "qkb": np.stack([w[p + "b"].reshape(DC, P).T for p in "qk"], 1), "vb": w["vb"], "ob": w["ob"],
        "ident": np.eye(P, dtype=np.float32),
        "keypos": keypos,
        "expert": (at // R).astype(np.float32).reshape(P, 1),
        "rowcoef": rowcoef,
    }
    nc = bacc.Bacc("TRN2", target_bir_lowering=False, num_devices=1)
    arrays, aps = {}, {}
    for name, a in ins.items():
        a = np.ascontiguousarray(a)
        arrays[f"in_{name}"] = a
        aps[name] = nc.dram_tensor(f"in_{name}", a.shape, mybir.dt.from_np(a.dtype), kind="ExternalInput").ap()
    out = nc.dram_tensor("out", (B, S, D), F32, kind="ExternalOutput").ap()
    v1_kept_hbm = nc.dram_tensor("v1_kept_hbm", (B, NK, D), F32, kind="Internal").ap()
    cross_and_mixture_attention(nc, **aps, out=out, v1_kept_hbm=v1_kept_hbm)
    return run_bass_kernel_spmd(nc, [arrays], core_ids=[0]).results[0]["out"]
```

```python
from contextlib import ExitStack

import concourse.bass as bass
from concourse import mybir

ALU = mybir.AluOpType
ACT = mybir.ActivationFunctionType
AX = mybir.AxisListType
F32 = mybir.dt.float32
F32R = mybir.dt.float32r
I32 = mybir.dt.int32
U32 = mybir.dt.uint32

P = 128
B, S, D = 8, 512, 512
H, DH = 16, 32
NK = 77
NKP = NK + 1
E, R = 8, 16
DC = D // P
TT = S // P
HJ = H // DC
SCALE = float(DH) ** -0.5
MASKED = -1e20 * float(DH) ** 0.5
EPS = 1e-5
MASK_ROW, SHIFT_ROW = 3 * DH, 3 * DH + 1
ROWS = SHIFT_ROW + 2
QP, KP, VP, OP = range(4)

CROSS, MIX = 0, 1


def score_tiles(half):
    return TT if half == CROSS else TT * HJ


def scores_fill(half, job):
    return ("scores", half, job, 0, score_tiles(half)) if half is not None else None


def between(half, job, after):
    steps = [("shift", half, job), ("norm",)]
    if after is not None and after[0] == MIX:
        steps += [("proj", *after, 0, None), ("proj", *after, 1, ("scoresT", half, job) if half == MIX else None)]
    elif after is not None:
        steps += [("proj", *after, 0, None)]
    return steps


def attend(half, job, then):
    early = half == MIX and 1 <= job <= 2
    return [("attend", half, job, early, scores_fill(*then))]


CROSS_START = [("proj", CROSS, 0, 0, None), ("proj", CROSS, 1, 0, None),
               ("only", scores_fill(CROSS, 0)), ("shift", CROSS, 0)]
CROSS_REST = [
    *attend(CROSS, 0, (CROSS, 1)), *between(CROSS, 1, (CROSS, 2)),
    *attend(CROSS, 1, (CROSS, 2)), *between(CROSS, 2, (CROSS, 3)),
    *attend(CROSS, 2, (CROSS, 3)), ("shift", CROSS, 3), ("norm",)]
MIX_START = [("weff", QP), ("weff", KP), ("proj", MIX, 0, 0, None), ("proj", MIX, 0, 1, None), ("weff", VP),
             ("vproj", ("scores", MIX, 0, 0, 12)), ("proj", MIX, 1, 0, ("scores", MIX, 0, 12, 16)),
             ("shift", MIX, 0), ("proj", MIX, 1, 1, None),
             *attend(MIX, 0, (MIX, 1)), *between(MIX, 1, (MIX, 2))]
PROLOGUE = ([("load",), ("context",), ("ln1",), ("keys1",), ("xpose",)] + CROSS_START + CROSS_REST
            + attend(CROSS, 3, (None, None))
            + [("norm",), ("out1",), ("ln2",), ("xpose",), ("pooled",), ("gate_hidden",), ("gate_top",),
               ("residual",)])
BODY = (MIX_START + [("load",)]
        + attend(MIX, 1, (MIX, 2)) + between(MIX, 2, (MIX, 3)) + [("ln1",), ("keys1",)]
        + attend(MIX, 2, (MIX, 3)) + [("shift", MIX, 3), ("norm",), ("xpose",), ("proj", CROSS, 0, 0, None)]
        + attend(MIX, 3, (CROSS, 0)) + [("shift", CROSS, 0), ("norm",), ("proj", CROSS, 1, 0, None)]
        + CROSS_REST + [("weff", OP)] + attend(CROSS, 3, (None, None))
        + [("norm",), ("out2", 0), ("out1",), ("ln2",), ("out2", 1), ("xpose",), ("pooled",), ("out2", 2),
           ("gate_hidden",), ("gate_top",), ("out2", 3), ("residual",)])
EPILOGUE = (MIX_START + attend(MIX, 1, (MIX, 2)) + between(MIX, 2, (MIX, 3)) + attend(MIX, 2, (MIX, 3))
            + [("shift", MIX, 3), ("norm",), ("weff", OP)] + attend(MIX, 3, (None, None)) + [("norm",)]
            + [("out2", t) for t in range(TT)])

BANK_USES = {"context": "D" * (2 * DC + B), "xpose": "A" * TT, "weff": "D" * DC, "vproj": "D" * TT,
             "shift": "D", "out1": "D" * TT, "out2": "D", "gate_hidden": "A", "gate_top": "D"}


def bank_uses(step):
    return "D" if step[0] == "proj" else BANK_USES.get(step[0], "")


def fill_of(step):
    return step[-1] if isinstance(step[-1], tuple) else None


def increments(step):
    name, uses = step[0], bank_uses(step)
    n = {"bank_full": len(uses), "act_evacuated": uses.count("A"), "dve_evacuated": uses.count("D")}
    if name == "load":
        n |= {"x_loaded": 16, "v1_loaded": 16}
    if name == "context":
        n |= {"v1_kept": 16 * B}
    if name == "keys1":
        n |= {"keys1_step": 6 + 2 * HJ}
    if name in ("ln1", "ln2"):
        n |= {"ln_step": 2 * TT + 1, "rstd_ready": 1, "xhat_ready": TT}
    if name == "proj":
        n |= {"hi_done": HJ, "dup_done": 1, "lo_step": HJ - 1}
    if name == "norm":
        n |= {"sum_inverted": 1, "normed": 1}
    fill = fill_of(step)
    if fill and fill[0] == "scores":
        n |= {"scores_full": fill[4] - fill[3], "rowmax_done": fill[4] - fill[3]}
    if fill and fill[0] == "scoresT":
        n |= {"scoresT_full": HJ, "exp_done": HJ}
    if name == "shift":
        n |= {"shift_hi": 1, "shift_moved": 32}
    if name == "attend":
        keys = S // P if step[1] == MIX else 1
        n |= {"scoresT_full": HJ * (keys - step[3]), "exp_done": HJ * (keys - step[3]), "pv_done": keys}
    if name == "weff":
        n |= {f"wm_loaded{dc}": 16 for dc in range(DC)} | {"vs_ready": int(step[1] != OP)}
    if name == "gate_top":
        n |= {"vs_ready": 1, "gate_step": 11, "gate_exp": 1}
    if name in ("gate_hidden", "pooled"):
        n |= {"gate_step": 1}
    if name == "residual":
        n |= {"residual_kept": TT}
    if name == "out2":
        n |= {"out_stored": 16}
    return n


def totals(steps):
    n = {}
    for step in steps:
        for key, k in increments(step).items():
            n[key] = n.get(key, 0) + k
    return n


class Count:

    def __init__(self, base, each=None, b=0):
        self.base, self.each, self.b, self.here = base, each or {}, b, {}

    def at(self, name, k=0):
        k += self.here.get(name, 0) + self.base.get(name, 0)
        return self.b * self.each[name] + k if self.each.get(name) else k

    def some(self, name, k=0):
        return self.at(name, k) >= 1 if not self.each else True

    def advance(self, step):
        for name, k in increments(step).items():
            self.here[name] = self.here.get(name, 0) + k


class Banks:

    def __init__(self, before):
        self.last = before
        self.n = 0

    def next(self, engine, at, used):
        waits = []
        if len(self.last) == 2:
            who = self.last[0]
            late = 1 if self.last[1] == who else 0
            names = {"A": ["act_evacuated"], "D": ["dve_evacuated"],
                     "*": ["act_evacuated", "dve_evacuated"]}[who]
            waits = [(name, at(name, 0 if who == "*" else used[who] - late)) for name in names]
        self.last = (self.last + engine)[-2:]
        used[engine] += 1
        self.n += 1
        return (self.n - 1) % 2, waits


def uses_of(steps):
    return "".join(bank_uses(step) for step in steps)


assert len(uses_of(PROLOGUE)) % 2 == 0 and len(uses_of(BODY)) % 2 == 0


def cross_and_mixture_attention(nc, x, ctxT, lens, Wq1, Wk1, Wv1, Wo1, gw1T, gb1, gw2T, gb2,
                                WmT, U, V, SV, qkb, vb, ob, ident, keypos, expert, rowcoef, out, v1_kept_hbm):
    ctx = ExitStack()
    with ctx:
        def sb(name, shape, dt=F32):
            return ctx.enter_context(nc.sbuf_tensor(name, shape, dt))

        def sem(name):
            return ctx.enter_context(nc.semaphore(name))

        Wq1_sb = sb("Wq1_sb", [P, DC, D])
        Wo1_sb = sb("Wo1_sb", [P, DC, D])
        U_sb = sb("U_sb", [P, 4, D])
        V_sb = sb("V_sb", [P, 4, D])
        SV_sb = sb("SV_sb", [P, 4])
        gw1T_sb = sb("gw1T_sb", [P, DC, P])
        gw2T_sb = sb("gw2T_sb", [P, E])
        gb1_sb = sb("gb1_sb", [P, 1])
        gb2_sb = sb("gb2_sb", [P, E])
        qkb_sb = sb("qkb_sb", [P, 2, DC])
        vb_sb = sb("vb_sb", [P, D])
        ob_sb = sb("ob_sb", [P, D])
        ident_sb = sb("ident_sb", [P, P])
        ones = sb("ones", [P, P])
        minus_half = sb("minus_half", [P, TT])
        expert_sb = sb("expert_sb", [P, 1])
        K1T = sb("K1T", [P, DC, B * NK])
        mask_rows = sb("mask_rows", [P, B, NKP])

        x1 = sb("x1", [P, TT, D])
        kept = sb("kept", [P, TT, D])
        xhat = sb("xhat", [P, TT, D])
        XT = sb("XT", [P, DC, S])
        wm_ring = sb("wm_ring", [P, DC, D])
        vs = sb("vs", [P, 2, D])
        Wqk = sb("Wqk", [P, 2, DC, D])
        Wvo = sb("Wvo", [P, DC, D])
        keys1 = sb("keys1", [P, DC, HJ, NKP], F32R)
        k1_hi = sb("k1_hi", [P, DC, NK], F32R)
        k1_lo = sb("k1_lo", [P, DC, NK], F32R)
        V1 = sb("V1", [P, D])
        V2 = sb("V2", [P, TT, D])
        ctx1T = sb("ctx1T", [P, DC, S])
        ctx2T = sb("ctx2T", [P, DC, S])

        qs = sb("qs", [P, 2, HJ, S], F32R)
        ks = sb("ks", [P, 2, HJ, S], F32R)
        probs = sb("probs", [P, 2 * HJ, S])
        inv_sum = sb("inv_sum", [P, S])
        negmax = sb("negmax", [P, P])
        shift = sb("shift", [HJ * TT, 2, P], F32R)

        bn = sb("bn", [P, TT, 6])
        meanvar = sb("meanvar", [P, TT, 2])
        vareps = sb("vareps", [P, TT])
        rstd = sb("rstd", [P, TT])
        pooled = sb("pooled", [P, DC])
        hidden = sb("hidden", [P, 1])
        hiddenB = sb("hiddenB", [P, P])
        logits = sb("logits", [P, E])
        top = sb("top", [P, 8])
        top_at = sb("top_at", [P, 8], U32)
        g = sb("g", [P, 16])
        sel = sb("sel", [P, 2])
        carrier = sb("carrier", [P, 1])
        lens_i = sb("lens_i", [P, B], I32)
        lens_f = sb("lens_f", [P, B])
        keypos_sb = sb("keypos_sb", [P, NKP])
        rowcoef_sb = sb("rowcoef_sb", [P, 2])

        ctxT_sb = probs[:, 0:5, :].rearrange("p a n -> p (a n)")[:, 0:DC * B * NK].rearrange(
            "p (c n) -> p c n", c=DC)
        valid = ks_valid = kept[:, 0:2, :].rearrange("p a n -> p (a n)")[:, 0:B * NKP].rearrange(
            "p (b n) -> p b n", b=B)
        Wk1_sb, Wv1_sb = Wqk[:, 1], Wvo

        def bank(name, n):
            return ctx.enter_context(nc.psum_tensor(name, [P, n, 512], F32))

        pj = bank("pj", 2)
        sc = bank("sc", 2)
        scT = bank("scT", 2)
        acc = bank("acc", 1)
        den = bank("den", 1)

        names = sorted({k for s in (PROLOGUE, BODY, EPILOGUE) for k in totals(s)})
        sems = {name: sem(name) for name in names}
        weights_loaded = sem("weights_loaded")
        context_loaded = sem("context_loaded")
        consts_loaded = sem("consts_loaded")
        consts_made = sem("consts_made")
        mask_step = sem("mask_step")

        def walk(engine, loop, handlers):
            pro, each = totals(PROLOGUE), totals(BODY)

            def segment(steps, count, before):
                banks = Banks(before)
                for step in steps:
                    if step[0] in handlers:
                        handlers[step[0]](count, step, banks)
                    elif bank_uses(step):
                        banks.last = (banks.last + bank_uses(step))[-2:]
                        banks.n += len(bank_uses(step))
                    count.advance(step)

            def row(n):
                return n

            c = Count({})
            c.row, c.ahead = None, row(0)
            segment(PROLOGUE, c, "")
            with loop(0, B - 1) as b:
                c = Count(pro, each, b)
                c.row, c.ahead = b, b + 1
                segment(BODY, c, "**")
            c = Count({k: pro.get(k, 0) + (B - 1) * each.get(k, 0) for k in {**pro, **each}})
            c.row, c.ahead = B - 1, None
            segment(EPILOGUE, c, "**")

        def rows(start, n):
            return slice(start, start + n) if isinstance(start, int) else bass.ds(start, n)

        block = ctx.enter_context(nc.Block())

        @block.sync
        def _(sp):
            for dst, src in ((ctxT_sb, ctxT.rearrange("(c p) n -> p c n", p=P)),
                             (Wk1_sb, Wk1.rearrange("(c p) n -> p c n", p=P))):
                sp.dma_start(dst, src).then_inc(context_loaded, 16)
            for dst, src in ((keypos_sb[:], keypos), (lens_i[:], lens.rearrange("(a n) -> a n", a=1)
                                                      .to_broadcast([P, B])),
                             (rowcoef_sb[:], rowcoef), (ident_sb[:], ident)):
                sp.dma_start(dst, src).then_inc(consts_loaded, 16)
            sp.dma_start(Wv1_sb[:], Wv1.rearrange("(c p) n -> p c n", p=P)).then_inc(context_loaded, 16)

            def load(c, step, banks):
                if c.row is not None:
                    sp.wait_ge(sems["residual_kept"], c.at("residual_kept"))
                    sp.wait_ge(sems["pv_done"], c.at("pv_done"))
                sp.dma_start(x1[:], x[rows(c.ahead, 1)].rearrange("a (t p) d -> p (a t) d", p=P))\
                  .then_inc(sems["x_loaded"], 16)
                if c.row is not None:
                    sp.dma_start(V1[0:NK, :], v1_kept_hbm[rows(c.ahead, 1)].rearrange("a k d -> k (a d)"))\
                      .then_inc(sems["v1_loaded"], 16)

            def context(c, step, banks):
                for dst, src in ((Wq1_sb[:], Wq1.rearrange("(c p) n -> p c n", p=P)),
                                 (Wo1_sb[:], Wo1.rearrange("(c p) n -> p c n", p=P)),
                                 (U_sb[:], U), (V_sb[:], V), (SV_sb[:], SV),
                                 (gw1T_sb[:], gw1T.rearrange("(c p) n -> p c n", p=P)),
                                 (gw2T_sb[:], gw2T), (gb1_sb[:], gb1.rearrange("(p a) -> p a", a=1)),
                                 (gb2_sb[:], gb2.rearrange("(a n) -> a n", a=1).to_broadcast([P, E])),
                                 (qkb_sb[:], qkb),
                                 (vb_sb[:], vb.rearrange("(a n) -> a n", a=1).to_broadcast([P, D])),
                                 (ob_sb[:], ob.rearrange("(a n) -> a n", a=1).to_broadcast([P, D])),
                                 (expert_sb[:], expert)):
                    sp.dma_start(dst, src).then_inc(weights_loaded, 16)
                for dc in range(DC):
                    sp.dma_start(wm_ring[:, dc, :], WmT[QP, dc * P:(dc + 1) * P, :])\
                      .then_inc(sems[f"wm_loaded{dc}"], 16)
                for b in range(B):
                    sp.wait_ge(sems["dve_evacuated"], c.at("dve_evacuated", 2 * DC + b + 1))
                    sp.dma_start(v1_kept_hbm[b], xhat[0:NK, b % TT, :]).then_inc(sems["v1_kept"], 16)
                sp.wait_ge(sems["v1_kept"], 16 * B)
                sp.dma_start(V1[0:NK, :], v1_kept_hbm[0]).then_inc(sems["v1_loaded"], 16)

            def weff(c, step, banks):
                nxt = (step[1] + 1) % 4
                if step[1] == OP and c.ahead is None:
                    return
                for dc in range(DC):
                    sp.wait_ge(sems["dve_evacuated"], c.at("dve_evacuated", dc + 1))
                    sp.dma_start(wm_ring[:, dc, :], WmT[nxt, dc * P:(dc + 1) * P, :])\
                      .then_inc(sems[f"wm_loaded{dc}"], 16)

            def move_shift(c, step, banks):
                sp.wait_ge(sems["dve_evacuated"], c.at("dve_evacuated", 1))
                for part in range(2):
                    row = SHIFT_ROW + part
                    sp.dma_start(qs[row:row + 1, step[2] % 2, :, :].rearrange("p j (t n) -> p (j t) n", n=P)
                                 .bitcast(F32), shift[:, part, :].bitcast(F32))\
                      .then_inc(sems["shift_moved"], 16)

            def out2(c, step, banks):
                t = step[1]
                sp.wait_ge(sems["dve_evacuated"], c.at("dve_evacuated", 1))
                sp.dma_start(out[rows(c.row, 1), t * P:(t + 1) * P, :].rearrange("a p d -> p (a d)"),
                             kept[:, t, :]).then_inc(sems["out_stored"], 16)

            walk(sp, sp.Fori, {"load": load, "context": context, "weff": weff, "shift": move_shift,
                               "out2": out2})
            sp.wait_ge(sems["out_stored"], 16 * B * TT)

        @block.gpsimd
        def _(pool):
            for n, (what, value) in enumerate((
                    (ones[:], 1.0), (minus_half[:], -0.5), (negmax[:], 0.0),
                    (qs[MASK_ROW:MASK_ROW + 1, :, :, :].bitcast(F32), 1.0),
                    (ks[MASK_ROW:ROWS, :, :, :].bitcast(F32), 1.0),
                    (ks[MASK_ROW:MASK_ROW + 1, :, :, :].bitcast(F32), 0.0))):
                nc.gpsimd.memset(what, value).then_inc(consts_made, 1)
                pool.wait_ge(consts_made, n + 1)

            def inverse_deviation(c, step, banks):
                pool.wait_ge(sems["ln_step"], c.at("ln_step", 2 * TT + 1))
                if c.row is not None or step[0] == "ln2":
                    pool.wait_ge(sems["xhat_ready"], c.at("xhat_ready"))
                nc.gpsimd.tensor_tensor(rstd[:], vareps[:], minus_half[:], ALU.pow)\
                    .then_inc(sems["rstd_ready"], 1)

            def residual(c, step, banks):
                pool.wait_ge(sems["dve_evacuated"], c.at("dve_evacuated"))
                if c.row is None:
                    pool.wait_ge(weights_loaded, 16 * 13)
                else:
                    pool.wait_ge(sems["out_stored"], c.at("out_stored"))
                for t in range(TT):
                    nc.gpsimd.tensor_tensor(kept[:, t, :], x1[:, t, :], ob_sb[:], ALU.add)\
                        .then_inc(sems["residual_kept"], 1)

            walk(pool, pool.Fori, {"ln1": inverse_deviation, "ln2": inverse_deviation,
                                   "residual": residual})

        @block.scalar
        def _(act):
            def xpose(c, step, banks):
                for t in range(TT):
                    p, _ = banks.next("A", c.at, {"A": 0, "D": 0})
                    act.wait_ge(sems["bank_full"], c.at("bank_full", t + 1))
                    nc.scalar.activation(XT[:, :, t * P:(t + 1) * P],
                                         pj[:, p, :].rearrange("p (c n) -> p c n", c=DC),
                                         ACT.Copy).then_inc(sems["act_evacuated"], 1)

            def exponentials(c, half, job, kt, done):
                keys = P if half == MIX else NK
                side = (kt if half == MIX else job) % 2
                read = kt - 1
                if c.some("pv_done", read):
                    act.wait_ge(sems["pv_done"], c.at("pv_done", read))
                for j in range(HJ):
                    act.wait_ge(sems["scoresT_full"], c.at("scoresT_full", done + j + 1))
                    nc.scalar.activation(probs[0:keys, side * HJ + j, :], scT[0:keys, j % 2, :],
                                         ACT.Exp, scale=SCALE).then_inc(sems["exp_done"], 1)

            def proj(c, step, banks):
                _, half, job, w, fill = step
                slot = job % 2
                if fill and fill[0] == "scoresT":
                    exponentials(c, fill[1], fill[2], 0, 0)
                stack = (qs, ks)[w]
                p, _ = banks.next("D", c.at, {"A": 0, "D": 0})
                act.wait_ge(sems["bank_full"], c.at("bank_full", 1))
                for j in range(HJ):
                    src = pj[j * DH:(j + 1) * DH, p, :]
                    dst = stack[0:DH, slot, j, :]
                    if half == MIX:
                        ins = nc.scalar.activation(dst, src, ACT.Identity,
                                                   bias=qkb_sb[j * DH:(j + 1) * DH, w, job:job + 1])
                    else:
                        ins = nc.scalar.activation(dst, src, ACT.Copy)
                    ins.then_inc(sems["hi_done"], 1)
                act.wait_ge(sems["hi_done"], c.at("hi_done", HJ))
                at = (DH, 2 * DH)[w]
                nc.scalar.activation(stack[at:at + DH, slot, :, :],
                                     stack[0:DH, slot, :, :].bitcast(F32), ACT.Copy)\
                    .then_inc(sems["dup_done"], 1)

            def attend(c, step, banks):
                _, half, job, early, _ = step
                for kt in range(int(early), TT if half == MIX else 1):
                    exponentials(c, half, job, kt, HJ * (kt - early))

            def gate_hidden(c, step, banks):
                p, _ = banks.next("A", c.at, {"A": 0, "D": 0})
                if c.row is None:
                    act.wait_ge(weights_loaded, 16 * 13)
                act.wait_ge(sems["bank_full"], c.at("bank_full", 1))
                nc.scalar.activation(hidden[:], pj[:, p, 0:1], ACT.Relu, bias=gb1_sb[:], scale=1.0 / S)\
                    .then_inc(sems["act_evacuated"], 1)

            def gate_top(c, step, banks):
                act.wait_ge(sems["gate_step"], c.at("gate_step", 4))
                nc.scalar.activation(g[:, 1:2], g[:, 0:1], ACT.Exp).then_inc(sems["gate_exp"], 1)

            walk(act, act.Fori, {"xpose": xpose, "proj": proj, "attend": attend,
                                 "gate_hidden": gate_hidden, "gate_top": gate_top})

        @block.vector
        def _(dve):
            def settle(semaphore, value):
                dve.wait_ge(semaphore, value)
                nc.vector.memset(carrier[:], 0.0)

            last_attended = None

            dve.wait_ge(consts_loaded, 64)
            nc.vector.tensor_copy(lens_f[:], lens_i[:]).then_inc(mask_step, 1)
            dve.wait_ge(mask_step, 1)
            for b in range(B):
                nc.vector.tensor_scalar(valid[:, b, :], keypos_sb[:], lens_f[:, b:b + 1], None, ALU.is_lt)\
                    .then_inc(mask_step, 1)
            dve.wait_ge(mask_step, B + 1)
            nc.vector.tensor_scalar(mask_rows[MASK_ROW:ROWS, :, :], valid[MASK_ROW:ROWS, :, :],
                                    rowcoef_sb[MASK_ROW:ROWS, 0:1], rowcoef_sb[MASK_ROW:ROWS, 1:2],
                                    ALU.mult, ALU.add).then_inc(mask_step, 1)
            dve.wait_ge(mask_step, B + 2)

            def context(c, step, banks):
                n = 0
                for co in range(DC):
                    for half in range(2):
                        p, _ = banks.next("D", c.at, {"A": 0, "D": 0})
                        n += 1
                        dve.wait_ge(sems["bank_full"], n)
                        nc.vector.tensor_tensor(
                            K1T[:, co, half * 4 * NK:(half + 1) * 4 * NK].rearrange("p (b k) -> p b k", k=NK),
                            pj[:, p, 0:4 * NK].rearrange("p (b k) -> p b k", k=NK),
                            valid[:, 4 * half:4 * half + 4, 0:NK], ALU.mult)\
                            .then_inc(sems["dve_evacuated"], 1)
                for b in range(B):
                    p, _ = banks.next("D", c.at, {"A": 0, "D": 0})
                    n += 1
                    dve.wait_ge(sems["bank_full"], n)
                    if b >= TT:
                        dve.wait_ge(sems["v1_kept"], 16 * TT)
                    nc.vector.tensor_copy(xhat[0:NK, b % TT, :], pj[0:NK, p, :])\
                        .then_inc(sems["dve_evacuated"], 1)

            def keys1_stack(c, step, banks):
                done = 0

                def then(ins):
                    nonlocal done
                    done += 1
                    ins.then_inc(sems["keys1_step"], 1)

                if c.row is None:
                    dve.wait_ge(sems["dve_evacuated"], c.at("dve_evacuated"))
                else:
                    dve.wait_ge(sems["pv_done"], c.at("pv_done", -1))
                src = K1T[:, :, rows(c.ahead * NK, NK)]
                then(nc.vector.tensor_copy(k1_hi[:], src))
                then(nc.vector.tensor_copy(keys1[MASK_ROW:ROWS, :, :, :].rearrange("p c j k -> p (c j) k"),
                                           mask_rows[MASK_ROW:ROWS, rows(c.ahead, 1), :]
                                           .to_broadcast([ROWS - MASK_ROW, H, NKP])))
                dve.wait_ge(sems["keys1_step"], c.at("keys1_step", done))
                then(nc.vector.tensor_tensor(k1_lo[:], src, k1_hi[:].bitcast(F32), ALU.subtract))
                if c.row is None:
                    nc.vector.memset(keys1[0:3 * DH, :, :, NK:NKP].bitcast(F32), 0.0).then_inc(mask_step, 1)
                for j in range(HJ):
                    then(nc.vector.tensor_copy(keys1[0:DH, :, j, 0:NK],
                                               k1_hi[j * DH:(j + 1) * DH].bitcast(F32)))
                dve.wait_ge(sems["keys1_step"], c.at("keys1_step", done))
                for j in range(HJ):
                    then(nc.vector.tensor_copy(keys1[DH:2 * DH, :, j, 0:NK],
                                               k1_lo[j * DH:(j + 1) * DH].bitcast(F32)))
                for half in range(3):
                    a, b = ((0, 2), (2, 3), (3, 4))[half]
                    then(nc.vector.tensor_copy(keys1[2 * DH:3 * DH, a:b, :, 0:NK],
                                               keys1[0:DH, a:b, :, 0:NK].bitcast(F32)))

            def layernorm(c, step, banks):
                for t in range(TT):
                    if step[0] == "ln1":
                        if t == 0:
                            dve.wait_ge(sems["x_loaded"], c.at("x_loaded"))
                    else:
                        dve.wait_ge(sems["dve_evacuated"], c.at("dve_evacuated", t + 1 - TT))
                    nc.vector.bn_stats(bn[:, t, :], x1[:, t, :]).then_inc(sems["ln_step"], 1)
                settle(sems["ln_step"], c.at("ln_step", TT))
                for t in range(TT):
                    nc.vector.bn_aggr(meanvar[:, t, :], bn[:, t, :]).then_inc(sems["ln_step"], 1)
                dve.wait_ge(sems["ln_step"], c.at("ln_step", 2 * TT))
                nc.vector.tensor_scalar(vareps[:], meanvar[:, :, 1], EPS, None, ALU.add)\
                    .then_inc(sems["ln_step"], 1)
                dve.wait_ge(sems["rstd_ready"], c.at("rstd_ready", 1))
                dve.wait_ge(sems["bank_full"], c.at("bank_full"))
                if c.row is None and step[0] == "ln1":
                    dve.wait_ge(sems["v1_kept"], 16 * B)
                for t in range(TT):
                    nc.vector.tensor_scalar(xhat[:, t, :], x1[:, t, :], meanvar[:, t, 0:1], rstd[:, t:t + 1],
                                            ALU.subtract, ALU.mult).then_inc(sems["xhat_ready"], 1)

            def reduce_scores(c, fill, first, end):
                _, half, job, n0, _ = fill
                for n in range(n0 + first, n0 + end):
                    dve.wait_ge(sems["scores_full"], c.at("scores_full", n - n0 + 1))
                    if half == MIX:
                        out_, in_ = negmax[:, n:n + 1], sc[:, n % 2, :]
                    else:
                        out_ = negmax[:, n:HJ * TT:TT]
                        in_ = sc[:, n % 2, 0:HJ * NKP].rearrange("p (j k) -> p j k", j=HJ)
                    nc.vector.tensor_reduce(out_, in_, AX.X, ALU.max, negate=True)\
                        .then_inc(sems["rowmax_done"], 1)

            def reduce_all(c, step):
                fill = fill_of(step)
                if fill and fill[0] == "scores":
                    reduce_scores(c, fill, 0, fill[4] - fill[3])

            def only(c, step, banks):
                dve.wait_ge(consts_made, 6)
                reduce_all(c, step)

            def proj(c, step, banks):
                _, half, job, w, fill = step
                slot = job % 2
                reduce_all(c, step)
                stack = (qs, ks)[w]
                p, _ = banks.next("D", c.at, {"A": 0, "D": 0})
                at = (2 * DH, DH)[w]
                for j in range(HJ):
                    dve.wait_ge(sems["hi_done"], c.at("hi_done", j + 1))
                    src = pj[j * DH:(j + 1) * DH, p, :]
                    bias = qkb_sb[j * DH:(j + 1) * DH, w, job:job + 1] if half == MIX else 0.0
                    nc.vector.scalar_tensor_tensor(stack[at:at + DH, slot, j, :], src, bias,
                                                   stack[0:DH, slot, j, :].bitcast(F32),
                                                   ALU.add, ALU.subtract)\
                        .then_inc(sems["dve_evacuated" if j == HJ - 1 else "lo_step"], 1)

            def shift_parts(c, step, banks):
                p, _ = banks.next("D", c.at, {"A": 0, "D": 0})
                dve.wait_ge(sems["bank_full"], c.at("bank_full", 1))
                if c.some("shift_moved"):
                    dve.wait_ge(sems["shift_moved"], c.at("shift_moved"))
                nc.vector.tensor_copy(shift[:, 0, :], pj[0:HJ * TT, p, 0:P]).then_inc(sems["shift_hi"], 1)
                dve.wait_ge(sems["shift_hi"], c.at("shift_hi", 1))
                nc.vector.tensor_tensor(shift[:, 1, :], pj[0:HJ * TT, p, 0:P], shift[:, 0, :].bitcast(F32),
                                        ALU.subtract).then_inc(sems["dve_evacuated"], 1)

            def attend(c, step, banks):
                nonlocal last_attended
                last_attended = step[1], step[2]
                reduce_all(c, step)

            def norm(c, step, banks):
                half, job = last_attended
                dve.wait_ge(sems["pv_done"], c.at("pv_done"))
                if c.some("normed"):
                    dve.wait_ge(sems["normed"], c.at("normed"))
                nc.vector.reciprocal(inv_sum[:], den[:, 0, :]).then_inc(sems["sum_inverted"], 1)
                dve.wait_ge(sems["sum_inverted"], c.at("sum_inverted", 1))
                nc.vector.tensor_tensor((ctx1T, ctx2T)[half][:, job, :], acc[:, 0, :], inv_sum[:], ALU.mult)\
                    .then_inc(sems["normed"], 1)

            def scale_v(c, p, k):
                dve.wait_ge(sems["bank_full"], c.at("bank_full", k))
                nc.vector.tensor_scalar(vs[:, p % 2, :], V_sb[:, p, :], g[:, 10 + p:11 + p], None, ALU.mult)\
                    .then_inc(sems["vs_ready"], 1)

            def weff(c, step, banks):
                p = step[1]
                if p != OP:
                    scale_v(c, p + 1, 0)
                dst = Wvo if p in (VP, OP) else Wqk[:, p]
                for dc in range(DC):
                    b, _ = banks.next("D", c.at, {"A": 0, "D": 0})
                    dve.wait_ge(sems[f"wm_loaded{dc}"], c.at(f"wm_loaded{dc}", 16))
                    dve.wait_ge(sems["bank_full"], c.at("bank_full", dc + 1))
                    nc.vector.tensor_tensor(dst[:, dc, :], pj[:, b, :], wm_ring[:, dc, :], ALU.add)\
                        .then_inc(sems["dve_evacuated"], 1)

            def vproj(c, step, banks):
                for t in range(TT):
                    p, _ = banks.next("D", c.at, {"A": 0, "D": 0})
                    reduce_scores(c, step[1], 3 * t, 3 * t + 3)
                    dve.wait_ge(sems["bank_full"], c.at("bank_full", t + 1))
                    nc.vector.tensor_tensor(V2[:, t, :], pj[:, p, :], vb_sb[:], ALU.add)\
                        .then_inc(sems["dve_evacuated"], 1)

            def out1(c, step, banks):
                for t in range(TT):
                    p, _ = banks.next("D", c.at, {"A": 0, "D": 0})
                    dve.wait_ge(sems["bank_full"], c.at("bank_full", t + 1))
                    nc.vector.tensor_tensor(x1[:, t, :], pj[:, p, :], x1[:, t, :], ALU.add)\
                        .then_inc(sems["dve_evacuated"], 1)

            def out2(c, step, banks):
                t = step[1]
                p, _ = banks.next("D", c.at, {"A": 0, "D": 0})
                dve.wait_ge(sems["residual_kept"], c.at("residual_kept"))
                dve.wait_ge(sems["bank_full"], c.at("bank_full", 1))
                nc.vector.tensor_tensor(kept[:, t, :], pj[:, p, :], kept[:, t, :], ALU.add)\
                    .then_inc(sems["dve_evacuated"], 1)

            def pool_tokens(c, step, banks):
                dve.wait_ge(sems["act_evacuated"], c.at("act_evacuated"))
                nc.vector.tensor_reduce(pooled[:], XT[:], AX.X, ALU.add).then_inc(sems["gate_step"], 1)

            def gate_hidden(c, step, banks):
                banks.next("A", c.at, {"A": 0, "D": 0})
                dve.wait_ge(sems["act_evacuated"], c.at("act_evacuated", 1))
                nc.vector.tensor_scalar(hiddenB[:], ones[:], hidden[:, 0:1], None, ALU.mult)\
                    .then_inc(sems["gate_step"], 1)

            def gate_top(c, step, banks):
                p, _ = banks.next("D", c.at, {"A": 0, "D": 0})
                n = 0

                def step_done(ins):
                    nonlocal n
                    n += 1
                    ins.then_inc(sems["gate_step"], 1)
                    wait = settle if n == 1 else dve.wait_ge
                    wait(sems["gate_step"], c.at("gate_step", n))

                dve.wait_ge(sems["bank_full"], c.at("bank_full", 1))
                nc.vector.tensor_tensor(logits[:], pj[:, p, 0:E], gb2_sb[:], ALU.add)\
                    .then_inc(sems["dve_evacuated"], 1)
                settle(sems["dve_evacuated"], c.at("dve_evacuated", 1))
                step_done(nc.vector.max(top[:], logits[:]))
                step_done(nc.vector.max_index(top_at[:], top[:], logits[:]))
                step_done(nc.vector.tensor_copy(g[:, 2:4], top_at[:, 0:2]))
                step_done(nc.vector.tensor_tensor(g[:, 0:1], top[:, 1:2], top[:, 0:1], ALU.subtract))
                dve.wait_ge(sems["gate_exp"], c.at("gate_exp", 1))
                step_done(nc.vector.tensor_scalar(g[:, 4:5], g[:, 1:2], 1.0, None, ALU.add))
                step_done(nc.vector.reciprocal(g[:, 5:6], g[:, 4:5]))
                step_done(nc.vector.tensor_tensor(g[:, 6:7], g[:, 5:6], g[:, 1:2], ALU.mult))
                step_done(nc.vector.tensor_scalar(sel[:], g[:, 2:4], expert_sb[:, 0:1], None, ALU.is_equal))
                step_done(nc.vector.tensor_tensor(g[:, 7:9], sel[:], g[:, 5:7], ALU.mult))
                step_done(nc.vector.tensor_tensor(g[:, 9:10], g[:, 7:8], g[:, 8:9], ALU.add))
                step_done(nc.vector.tensor_scalar(g[:, 10:14], SV_sb[:], g[:, 9:10], None, ALU.mult))
                scale_v(c, QP, 0)

            walk(dve, dve.Fori, {"context": context, "keys1": keys1_stack, "ln1": layernorm,
                                 "ln2": layernorm, "proj": proj, "only": only, "shift": shift_parts,
                                 "attend": attend, "norm": norm, "pooled": pool_tokens, "weff": weff, "vproj": vproj, "out1": out1,
                                 "out2": out2, "gate_hidden": gate_hidden, "gate_top": gate_top})

        @block.tensor
        def _(pe):
            pe.wait_ge(consts_loaded, 64)
            pe.wait_ge(consts_made, 6)

            def take(c, banks, engine, used):
                p, waits = banks.next(engine, c.at, used)
                for name, value in waits:
                    pe.wait_ge(sems[name], value)
                return p

            def context(c, step, banks):
                used = {"A": 0, "D": 0}
                pe.wait_ge(context_loaded, 48)
                for co in range(DC):
                    for half in range(2):
                        p = take(c, banks, "D", used)
                        for dc in range(DC):
                            mm = nc.tensor.matmul(pj[:, p, 0:4 * NK], Wk1_sb[:, dc, co * P:(co + 1) * P],
                                                  ctxT_sb[:, dc, half * 4 * NK:(half + 1) * 4 * NK],
                                                  start=(dc == 0), stop=(dc == DC - 1))
                        mm.then_inc(sems["bank_full"], 1)
                for b in range(B):
                    p = take(c, banks, "D", used)
                    for dc in range(DC):
                        mm = nc.tensor.matmul(pj[0:NK, p, :], ctxT_sb[:, dc, b * NK:(b + 1) * NK],
                                              Wv1_sb[:, dc, :], start=(dc == 0), stop=(dc == DC - 1))
                    mm.then_inc(sems["bank_full"], 1)

            def xpose(c, step, banks):
                used = {"A": 0, "D": 0}
                for t in range(TT):
                    p = take(c, banks, "A", used)
                    pe.wait_ge(sems["xhat_ready"], c.at("xhat_ready", t + 1 - TT))
                    for dc in range(DC):
                        mm = nc.tensor.transpose(pj[:, p, dc * P:(dc + 1) * P], xhat[:, t, dc * P:(dc + 1) * P],
                                                 ident_sb[:])
                    mm.then_inc(sems["bank_full"], 1)

            def stacks_ready(c, half):
                pe.wait_ge(sems["dve_evacuated"], c.at("dve_evacuated"))
                pe.wait_ge(sems["dup_done"], c.at("dup_done"))
                if half == CROSS:
                    pe.wait_ge(sems["keys1_step"], c.at("keys1_step"))

            def scores(c, fill, first, end):
                _, half, job, n0, n1 = fill
                slot = job % 2
                if first == 0:
                    stacks_ready(c, half)
                for n in range(n0 + first, min(n0 + end, n1)):
                    if c.some("rowmax_done", n - n0 - 1):
                        pe.wait_ge(sems["rowmax_done"], c.at("rowmax_done", n - n0 - 1))
                    if half == MIX:
                        j, t = n // TT, n % TT
                        nc.tensor.matmul(sc[:, n % 2, :], qs[0:3 * DH, slot, j, t * P:(t + 1) * P],
                                         ks[0:3 * DH, slot, j, :], start=True, stop=True)\
                            .then_inc(sems["scores_full"], 1)
                    else:
                        for j in range(HJ):
                            mm = nc.tensor.matmul(sc[:, n % 2, j * NKP:(j + 1) * NKP],
                                                  qs[0:MASK_ROW + 1, slot, j, n * P:(n + 1) * P],
                                                  keys1[0:MASK_ROW + 1, job, j, :], start=True, stop=True)
                        mm.then_inc(sems["scores_full"], 1)

            def scores_transposed(c, half, job, kt, j, done):
                slot = job % 2
                if kt == 0 and j == 0:
                    pe.wait_ge(sems["shift_moved"], c.at("shift_moved"))
                if c.some("exp_done", done - 1):
                    pe.wait_ge(sems["exp_done"], c.at("exp_done", done - 1))
                keys = P if half == MIX else NK
                lhsT = (ks[0:ROWS, slot, j, kt * P:(kt + 1) * P] if half == MIX
                        else keys1[0:ROWS, job, j, 0:NK])
                nc.tensor.matmul(scT[0:keys, j % 2, :], lhsT, qs[0:ROWS, slot, j, :],
                                 start=True, stop=True).then_inc(sems["scoresT_full"], 1)

            def only(c, step, banks):
                pe.wait_ge(mask_step, B + 3)
                scores(c, step[1], 0, score_tiles(step[1][1]))

            def proj(c, step, banks):
                _, half, job, w, fill = step
                if c.row is None:
                    pe.wait_ge(weights_loaded, 16 * 13)
                pe.wait_ge(sems["act_evacuated"], c.at("act_evacuated"))
                if half == MIX and job == 0:
                    pe.wait_ge(sems["dve_evacuated"], c.at("dve_evacuated", 0 if w == 0 else -1))
                p = take(c, banks, "D", {"A": 0, "D": 0})
                W = Wq1_sb if half == CROSS else Wqk[:, w]
                for dc in range(DC):
                    mm = nc.tensor.matmul(pj[:, p, :], W[:, dc, job * P:(job + 1) * P], XT[:, dc, :],
                                          start=(dc == 0), stop=(dc == DC - 1))
                    if dc == DC - 1:
                        mm.then_inc(sems["bank_full"], 1)
                    if fill and fill[0] == "scores":
                        scores(c, fill, dc, dc + 1)
                    if fill and fill[0] == "scoresT":
                        scores_transposed(c, fill[1], fill[2], 0, dc, dc)

            def turn_shift(c, step, banks):
                p = take(c, banks, "D", {"A": 0, "D": 0})
                pe.wait_ge(sems["rowmax_done"], c.at("rowmax_done"))
                nc.tensor.transpose(pj[:, p, 0:P], negmax[:], ident_sb[:]).then_inc(sems["bank_full"], 1)

            def p_times_v(c, half, job, kt, exps):
                keys, key_tiles = (P, TT) if half == MIX else (NK, 1)
                side = (kt if half == MIX else job) % 2
                pe.wait_ge(sems["exp_done"], c.at("exp_done", exps))
                if kt == 0:
                    if c.some("normed"):
                        pe.wait_ge(sems["normed"], c.at("normed"))
                    if half == CROSS:
                        pe.wait_ge(sems["v1_loaded"], c.at("v1_loaded"))
                for to in (acc, den):
                    for j in range(HJ):
                        head = (job * HJ + j) * DH
                        lhsT = (ones[0:keys, 0:DH] if to is den else
                                V2[:, kt, head:head + DH] if half == MIX else V1[0:NK, head:head + DH])
                        mm = nc.tensor.matmul(to[j * DH:(j + 1) * DH, 0, :], lhsT,
                                              probs[0:keys, side * HJ + j, :],
                                              start=(kt == 0), stop=(kt == key_tiles - 1))
                mm.then_inc(sems["pv_done"], 1)

            def attend(c, step, banks):
                _, half, job, early, fill = step
                key_tiles = TT if half == MIX else 1
                tiles = score_tiles(fill[1]) if fill else 0
                filled = 0

                def take_fill(until):
                    nonlocal filled
                    if fill and until > filled:
                        scores(c, fill, filled, until)
                        filled = until

                for kt in range(key_tiles + 1):
                    for half_of_heads in range(2):
                        if early <= kt < key_tiles:
                            for j in (2 * half_of_heads, 2 * half_of_heads + 1):
                                scores_transposed(c, half, job, kt, j, HJ * (kt - early) + j)
                        if kt or not early:
                            part = 2 * kt + half_of_heads + 1
                            take_fill(min(tiles, -(-tiles * part // (2 * key_tiles))))
                    if kt:
                        p_times_v(c, half, job, kt - 1, HJ * (kt - early))

            def weff(c, step, banks):
                p = step[1]
                used = {"A": 0, "D": 0}
                pe.wait_ge(sems["vs_ready"], c.at("vs_ready"))
                for dc in range(DC):
                    b = take(c, banks, "D", used)
                    nc.tensor.matmul(pj[:, b, :], vs[:, p % 2, dc * P:(dc + 1) * P], U_sb[:, p, :],
                                     start=True, stop=True).then_inc(sems["bank_full"], 1)

            def vproj(c, step, banks):
                used = {"A": 0, "D": 0}
                pe.wait_ge(sems["act_evacuated"], c.at("act_evacuated"))
                pe.wait_ge(sems["dve_evacuated"], c.at("dve_evacuated"))
                for t in range(TT):
                    p = take(c, banks, "D", used)
                    for dc in range(DC):
                        mm = nc.tensor.matmul(pj[:, p, :], XT[:, dc, t * P:(t + 1) * P], Wvo[:, dc, :],
                                              start=(dc == 0), stop=(dc == DC - 1))
                        if dc < DC - 1:
                            scores(c, step[1], 3 * t + dc, 3 * t + dc + 1)
                    mm.then_inc(sems["bank_full"], 1)

            def project_out(c, banks, used, srcT, W, t):
                p = take(c, banks, "D", used)
                for dc in range(DC):
                    mm = nc.tensor.matmul(pj[:, p, :], srcT[:, dc, t * P:(t + 1) * P], W[:, dc, :],
                                          start=(dc == 0), stop=(dc == DC - 1))
                mm.then_inc(sems["bank_full"], 1)

            def out1(c, step, banks):
                used = {"A": 0, "D": 0}
                pe.wait_ge(sems["normed"], c.at("normed"))
                for t in range(TT):
                    project_out(c, banks, used, ctx1T, Wo1_sb, t)

            def out2(c, step, banks):
                pe.wait_ge(sems["normed"], c.at("normed"))
                pe.wait_ge(sems["dve_evacuated"], c.at("dve_evacuated"))
                project_out(c, banks, {"A": 0, "D": 0}, ctx2T, Wvo, step[1])

            def gate_hidden(c, step, banks):
                p = take(c, banks, "A", {"A": 0, "D": 0})
                pe.wait_ge(sems["gate_step"], c.at("gate_step"))
                for dc in range(DC):
                    mm = nc.tensor.matmul(pj[:, p, 0:1], gw1T_sb[:, dc, :], pooled[:, dc:dc + 1],
                                          start=(dc == 0), stop=(dc == DC - 1))
                mm.then_inc(sems["bank_full"], 1)

            def gate_top(c, step, banks):
                p = take(c, banks, "D", {"A": 0, "D": 0})
                pe.wait_ge(sems["gate_step"], c.at("gate_step"))
                nc.tensor.matmul(pj[:, p, 0:E], hiddenB[:], gw2T_sb[:], start=True, stop=True)\
                    .then_inc(sems["bank_full"], 1)

            walk(pe, pe.Fori, {"context": context, "xpose": xpose, "proj": proj, "only": only,
                               "shift": turn_shift, "attend": attend, "weff": weff, "vproj": vproj,
                               "out1": out1, "out2": out2, "gate_hidden": gate_hidden,
                               "gate_top": gate_top})


def kernel(x, ctx_1024, _lenS2, L0_xattn_Wq, L0_xattn_Wk, L0_xattn_Wv, L0_xattn_Wo, **ffn):
    import numpy as np
    import concourse.bacc as bacc
    from concourse.bass_utils import run_bass_kernel_spmd

    w = {k.removeprefix("L0_ffn_"): np.asarray(v) for k, v in ffn.items()}
    at = np.arange(P)
    rowcoef = np.zeros((P, 2), np.float32)
    rowcoef[MASK_ROW] = (-MASKED, MASKED)
    rowcoef[SHIFT_ROW:ROWS] = (0.0, 1.0)
    keypos = np.full((P, NKP), 1e9, np.float32)
    keypos[:, :NK] = np.arange(NK)
    ins = {
        "x": x,
        "ctxT": np.asarray(ctx_1024).reshape(B * NK, D).T,
        "lens": np.asarray(_lenS2),
        "Wq1": L0_xattn_Wq, "Wk1": L0_xattn_Wk, "Wv1": L0_xattn_Wv, "Wo1": L0_xattn_Wo,
        "gw1T": w["gw1"].T, "gb1": w["gb1"], "gw2T": w["gw2"].T, "gb2": w["gb2"],
        "WmT": np.stack([w[p + "Wm"].T for p in "qkvo"]),
        "U": np.stack([w[p + "U"].transpose(0, 2, 1).reshape(E * R, D) for p in "qkvo"], 1),
        "V": np.stack([w[p + "V"].reshape(E * R, D) for p in "qkvo"], 1),
        "SV": np.stack([w[p + "S"].reshape(E * R) for p in "qkvo"], 1),
        "qkb": np.stack([w[p + "b"].reshape(DC, P).T for p in "qk"], 1), "vb": w["vb"], "ob": w["ob"],
        "ident": np.eye(P, dtype=np.float32),
        "keypos": keypos,
        "expert": (at // R).astype(np.float32).reshape(P, 1),
        "rowcoef": rowcoef,
    }
    nc = bacc.Bacc("TRN2", target_bir_lowering=False, num_devices=1)
    arrays, aps = {}, {}
    for name, a in ins.items():
        a = np.ascontiguousarray(a)
        arrays[f"in_{name}"] = a
        aps[name] = nc.dram_tensor(f"in_{name}", a.shape, mybir.dt.from_np(a.dtype), kind="ExternalInput").ap()
    out = nc.dram_tensor("out", (B, S, D), F32, kind="ExternalOutput").ap()
    v1_kept_hbm = nc.dram_tensor("v1_kept_hbm", (B, NK, D), F32, kind="Internal").ap()
    cross_and_mixture_attention(nc, **aps, out=out, v1_kept_hbm=v1_kept_hbm)
    return run_bass_kernel_spmd(nc, [arrays], core_ids=[0]).results[0]["out"]
```

```python
from contextlib import ExitStack

import concourse.bass as bass
from concourse import mybir

ALU = mybir.AluOpType
ACT = mybir.ActivationFunctionType
AX = mybir.AxisListType
F32 = mybir.dt.float32
F32R = mybir.dt.float32r
I32 = mybir.dt.int32
U32 = mybir.dt.uint32

P = 128
B, S, D = 8, 512, 512
H, DH = 16, 32
NK = 77
NKP = NK + 1
E, R = 8, 16
DC = D // P
TT = S // P
HJ = H // DC
SCALE = float(DH) ** -0.5
MASKED = -1e20 * float(DH) ** 0.5
EPS = 1e-5
MASK_ROW, SHIFT_ROW = 3 * DH, 3 * DH + 1
ROWS = SHIFT_ROW + 2
QP, KP, VP, OP = range(4)

CROSS, MIX = 0, 1


def score_tiles(half):
    return TT if half == CROSS else TT * HJ


def all_tiles(half, job):
    return half, job, 0, score_tiles(half)


LATE = 3
PLACES = {MIX: (0, 1, 2, 3, 3), CROSS: (0, 0, 1, 2, 4)}


def mix_cycle(job, tiles, q, k):
    return [("attend", MIX, job, tiles), *q, ("finish", MIX, job), *k]


def mix_then_mix(job):
    tiles = score_tiles(MIX)
    return mix_cycle(job, (MIX, job + 1, 0, tiles - LATE),
                     [("proj", MIX, job + 2, 0, None, (MIX, job + 1, tiles - LATE, tiles)),
                      ("shift", MIX, job + 1), ("lo", MIX, job + 2, 0)],
                     project(MIX, job + 2, 1, (MIX, job + 1)))


def project(half, job, w, early=None, tiles=None):
    return [("proj", half, job, w, early, tiles), ("lo", half, job, w)]


def cross_cycles(fill2, fill3):
    steps = []
    for job in (0, 1):
        proj, lo = project(CROSS, job + 2, 0, (CROSS, job), all_tiles(CROSS, job + 1))
        steps += [proj, ("shift", CROSS, job + 1), lo, ("finish", CROSS, job)]
    return steps + [*fill2, ("scores", all_tiles(CROSS, 3)), ("shift", CROSS, 3), ("finish", CROSS, 2),
                    *fill3, ("finish", CROSS, 3)]


MIX_START = [("weff", QP, None), ("weff", KP, None), ("weff", VP, None), ("proj", MIX, 0, 0, None, None),
             ("proj", MIX, 0, 1, None, None), ("lo", MIX, 0, 0), ("lo", MIX, 0, 1), ("load",), ("keys1",),
             ("vproj", all_tiles(MIX, 0)), ("shift", MIX, 0), ("proj", MIX, 1, 0, None, None), ("ln1",),
             ("lo", MIX, 1, 0), *project(MIX, 1, 1, (MIX, 0)), *mix_then_mix(0), *mix_then_mix(1)]
SECOND_HALF = [("out1",), ("ln2",), ("out2", 1, None), ("xpose", None), ("pooled",), ("out2", 2, None),
               ("gate_hidden",), ("gate_top",), ("out2", 3, None), ("residual",)]
PROLOGUE = ([("load",), ("context_keys",), ("ln1", "on VectorE"), ("keys1",), ("context_values",),
             ("xpose", None), *project(CROSS, 0, 0), *project(CROSS, 1, 0),
             ("scores", all_tiles(CROSS, 0)), ("shift", CROSS, 0)]
            + cross_cycles([("first", (CROSS, 2))], [("first", (CROSS, 3))])
            + [step for step in SECOND_HALF if step[0] != "out2"])
BODY = (MIX_START
        + mix_cycle(2, (MIX, 3, 0, score_tiles(MIX) - LATE),
                    [("xpose", (MIX, 3, score_tiles(MIX) - LATE, score_tiles(MIX))), ("shift", MIX, 3)],
                    project(CROSS, 0, 0, (MIX, 3)))
        + mix_cycle(3, all_tiles(CROSS, 0), [("shift", CROSS, 0), *project(CROSS, 1, 0)], [])
        + cross_cycles([("weff", OP, (CROSS, 2))], [("out2", 0, (CROSS, 3))])
        + SECOND_HALF)
EPILOGUE = ([step for step in MIX_START if step[0] not in ("load", "keys1", "ln1")]
            + mix_cycle(2, all_tiles(MIX, 3), [("shift", MIX, 3)], [("weff", OP, (MIX, 3))])
            + mix_cycle(3, None, [], []) + [("out2", t, None) for t in range(TT)])

CTX_TILES = [(at, min(at + P, B * NK)) for at in range(0, B * NK, P)]

BANK_USES = {"context_keys": "D" * (2 * DC), "context_values": "D" * len(CTX_TILES),
             "xpose": "A" * TT, "weff": "D" * DC, "vproj": "D" * TT,
             "out1": "D" * TT, "out2": "D", "gate_hidden": "A", "gate_top": "D", "proj": "L"}


def scores_within(step):
    return step[-1] if step[0] in ("scores", "vproj", "attend", "proj", "xpose") else None


def early_within(step):
    return step[4] if step[0] == "proj" else step[-1] if step[0] in ("weff", "out2", "first") else None


def bank_uses(step):
    return BANK_USES.get(step[0], "")


def increments(step):
    name, uses = step[0], bank_uses(step)
    n = {"bank_full": len(uses), "act_evacuated": uses.count("A"), "dve_evacuated": uses.count("D"),
         "lo_evacuated": uses.count("L")}
    if name == "load":
        n |= {"x_loaded": 16, "v1_loaded": 16}
    if name == "context_values":
        n |= {"v1_kept": 16 * len(CTX_TILES)}
    if name == "keys1":
        n |= {"keys1_hi": 1, "keys1_lo": 1, "keys1_stacked": 1 + 3 * HJ}
    if name == "ln1":
        n |= {"pool_settled": int(step == ("ln1",))}
    if name in ("ln1", "ln2"):
        n |= {"ln_step": TT + 1 + TT * (name == "ln1"), "rstd_ready": 1, "xhat_ready": TT}
    if name == "out1":
        n |= {"ln_step": TT}
    if name == "proj":
        slot = step[2] % 2
        n |= {"hi_done": HJ if step[3] == 0 else HJ // 2, "lo_step": HJ - 1}
        n |= {f"q_dup{slot}": 16} if step[3] == 0 else {f"k_dup{slot}_01": 16, f"k_dup{slot}_23": 16}
    if name == "lo" and step[3] == 1:
        n |= {"hi_by_dve": HJ // 2}
    if scores_within(step):
        tiles = scores_within(step)[3] - scores_within(step)[2]
        n |= {"scores_full": tiles, "rowmax_done": tiles}
    if early_within(step):
        n |= {"scoresT_full": HJ, "exp_done": HJ}
    if name == "shift":
        n |= {"shift_turned": 1, "shift_hi": 1, "shift_lo": 1, "shift_moved": 32}
    if name == "attend":
        n |= {"scoresT_full": HJ * (TT - 1), "exp_done": HJ * (TT - 1), "pv_done": TT - 1}
    if name == "finish":
        n |= {"pv_done": 1, "copied": 2, "sum_inverted": pieces(step[2]), "normed": pieces(step[2])}
    if name == "weff":
        n |= {f"wm_loaded{dc}": 16 for dc in range(DC)} | {"vs_ready": int(step[1] != OP)}
    if name == "gate_top":
        n |= {"vs_ready": 1, "gate_step": 11, "gate_exp": 1}
    if name == "gate_hidden":
        n |= {"gate_step": 1}
    if name == "pooled":
        n |= {"gate_step": TT + 1}
    if name == "residual":
        n |= {"residual_kept": TT}
    if name == "out2":
        n |= {"out_stored": 16}
    return n


def scores_by(place):
    skipped = DC - 1
    return max(0, -(-TT * HJ * (place - skipped) // (TT * (DC - 1) - skipped)))


def pieces(job):
    return TT if job == DC - 1 else 1


def totals(steps):
    n = {}
    for step in steps:
        for key, k in increments(step).items():
            n[key] = n.get(key, 0) + k
    return n


class Count:

    def __init__(self, base, each=None, b=0):
        self.base, self.each, self.b, self.here = base, each or {}, b, {}

    def at(self, name, k=0):
        k += self.here.get(name, 0) + self.base.get(name, 0)
        return self.b * self.each[name] + k if self.each.get(name) else k

    def some(self, name, k=0):
        return self.at(name, k) >= 1 if not self.each else True

    def advance(self, step):
        for name, k in increments(step).items():
            self.here[name] = self.here.get(name, 0) + k


class Banks:

    def __init__(self, before, first):
        self.last = before
        self.n = first

    def next(self, engine, at, used):
        waits = []
        if len(self.last) == 2:
            who = self.last[0]
            late = 1 if self.last[1] == who else 0
            names = {"A": ["act_evacuated"], "D": ["dve_evacuated"], "L": ["lo_evacuated"],
                     "*": ["act_evacuated", "dve_evacuated", "lo_evacuated"]}[who]
            waits = [(name, at(name, 0 if who == "*" else used[who] - late)) for name in names]
        self.last = (self.last + engine)[-2:]
        used[engine] += 1
        self.n += 1
        return (self.n - 1) % 2, waits


def no_uses():
    return {"A": 0, "D": 0, "L": 0}


def uses_of(steps):
    return "".join(bank_uses(step) for step in steps)


assert len(uses_of(BODY)) % 2 == 0


def cross_and_mixture_attention(nc, x, ctxT, lens, Wq1, Wk1, Wv1, Wo1, gw1T, gb1, gw2T, gb2,
                                WmT, U, V, SV, qkb, vb, ob, ident, keypos, expert, rowcoef, out, v1_kept_hbm):
    ctx = ExitStack()
    with ctx:
        def sb(name, shape, dt=F32):
            return ctx.enter_context(nc.sbuf_tensor(name, shape, dt))

        def sem(name):
            return ctx.enter_context(nc.semaphore(name))

        Wq1_sb = sb("Wq1_sb", [P, DC, D])
        Wo1_sb = sb("Wo1_sb", [P, DC, D])
        U_sb = sb("U_sb", [P, 4, D])
        V_sb = sb("V_sb", [P, 4, D])
        SV_sb = sb("SV_sb", [P, 4])
        gw1T_sb = sb("gw1T_sb", [P, DC, P])
        gw2T_sb = sb("gw2T_sb", [P, E])
        gb1_sb = sb("gb1_sb", [P, 1])
        gb2_sb = sb("gb2_sb", [P, E])
        qkb_sb = sb("qkb_sb", [P, 2, DC])
        vb_sb = sb("vb_sb", [P, D])
        ob_sb = sb("ob_sb", [P, D])
        ident_sb = sb("ident_sb", [P, P])
        ones = sb("ones", [P, P])
        minus_half = sb("minus_half", [P, TT])
        expert_sb = sb("expert_sb", [P, 1])
        K1T = sb("K1T", [P, DC, B * NK])
        mask_rows = sb("mask_rows", [P, B, NKP])

        x1 = sb("x1", [P, TT, D])
        kept = sb("kept", [P, TT, D])
        xhat = sb("xhat", [P, TT, D])
        XT = sb("XT", [P, DC, S])
        wm_ring = sb("wm_ring", [P, DC, D])
        vs = sb("vs", [P, 2, D])
        Wqk = sb("Wqk", [P, 2, DC, D])
        Wvo = sb("Wvo", [P, DC, D])
        keys1 = sb("keys1", [P, DC, HJ, NKP], F32R)
        k1_hi = sb("k1_hi", [P, DC, NK], F32R)
        k1_lo = sb("k1_lo", [P, DC, NK], F32R)
        V1 = sb("V1", [P, D])
        V2 = sb("V2", [P, TT, D])
        ctx1T = xhat
        ctx2T = sb("ctx2T", [P, DC, S])

        qs = sb("qs", [P, 2, HJ, S], F32R)
        ks = sb("ks", [P, 2, HJ, S], F32R)
        probs = sb("probs", [P, 2 * HJ, S])
        inv_sum = sb("inv_sum", [P, S])
        negmax = sb("negmax", [P, P])
        shift = sb("shift", [HJ * TT, 2, P], F32R)

        bn = sb("bn", [P, TT, 6])
        meanvar = sb("meanvar", [P, TT, 2])
        vareps = sb("vareps", [P, TT])
        rstd = sb("rstd", [P, TT])
        tile_sums = sb("tile_sums", [P, DC, TT])
        pooled = sb("pooled", [P, DC])
        hidden = sb("hidden", [P, 1])
        hiddenB = sb("hiddenB", [P, P])
        logits = sb("logits", [P, E])
        top = sb("top", [P, 8])
        top_at = sb("top_at", [P, 8], U32)
        g = sb("g", [P, 16])
        sel = sb("sel", [P, 2])
        carrier = sb("carrier", [P, 1])
        pool_carrier = sb("pool_carrier", [P, 1])
        lens_i = sb("lens_i", [P, B], I32)
        lens_f = sb("lens_f", [P, B])
        keypos_sb = sb("keypos_sb", [P, NKP])
        rowcoef_sb = sb("rowcoef_sb", [P, 2])

        ctxT_sb = probs[:, 0:5, :].rearrange("p a n -> p (a n)")[:, 0:DC * B * NK].rearrange(
            "p (c n) -> p c n", c=DC)
        valid = kept[:, 0:2, :].rearrange("p a n -> p (a n)")[:, 0:B * NKP].rearrange(
            "p (b n) -> p b n", b=B)
        Wk1_sb, Wv1_sb = Wqk[:, 1], Wvo

        def bank(name, n):
            return ctx.enter_context(nc.psum_tensor(name, [P, n, 512], F32))

        pj = bank("pj", 2)
        sc = bank("sc", 2)
        scT = bank("scT", 2)
        acc = bank("acc", 1)
        den = bank("den", 1)

        names = sorted({k for s in (PROLOGUE, BODY, EPILOGUE) for k in totals(s)})
        sems = {name: sem(name) for name in names}
        weights_loaded = sem("weights_loaded")
        context_loaded = sem("context_loaded")
        consts_loaded = sem("consts_loaded")
        consts_made = sem("consts_made")
        mask_step = sem("mask_step")

        def walk(engine, loop, handlers):
            pro, each = totals(PROLOGUE), totals(BODY)

            def segment(steps, count, before):
                banks = Banks(before, len(uses_of(steps)) % 2 if steps is PROLOGUE else 0)
                for step in steps:
                    if step[0] in handlers:
                        handlers[step[0]](count, step, banks)
                    elif bank_uses(step):
                        banks.last = (banks.last + bank_uses(step))[-2:]
                        banks.n += len(bank_uses(step))
                    count.advance(step)

            c = Count({})
            c.row, c.ahead = None, 0
            segment(PROLOGUE, c, "")
            with loop(0, B - 1) as b:
                c = Count(pro, each, b)
                c.row, c.ahead = b, b + 1
                segment(BODY, c, "**")
            c = Count({k: pro.get(k, 0) + (B - 1) * each.get(k, 0) for k in {**pro, **each}})
            c.row, c.ahead = B - 1, None
            segment(EPILOGUE, c, "**")

        def rows(start, n):
            return slice(start, start + n) if isinstance(start, int) else bass.ds(start, n)

        def normalize(engine):
            for t in range(TT):
                engine.tensor_scalar(xhat[:, t, :], x1[:, t, :], meanvar[:, t, 0:1], rstd[:, t:t + 1],
                                     ALU.subtract, ALU.mult).then_inc(sems["xhat_ready"], 1)

        def duplicate_keys(queue, slot, j):
            queue.dma_start(ks[2 * DH:3 * DH, slot, j:j + 2, :].bitcast(F32),
                            ks[0:DH, slot, j:j + 2, :].bitcast(F32))\
                 .then_inc(sems[f"k_dup{slot}_{j}{j + 1}"], 16)

        block = ctx.enter_context(nc.Block())

        @block.sync
        def _(sp):
            for dst, src in ((ctxT_sb, ctxT.rearrange("(c p) n -> p c n", p=P)),
                             (Wk1_sb, Wk1.rearrange("(c p) n -> p c n", p=P))):
                sp.dma_start(dst, src).then_inc(context_loaded, 16)
            for dst, src in ((keypos_sb[:], keypos), (lens_i[:], lens.rearrange("(a n) -> a n", a=1)
                                                      .to_broadcast([P, B])),
                             (rowcoef_sb[:], rowcoef), (ident_sb[:], ident)):
                sp.dma_start(dst, src).then_inc(consts_loaded, 16)
            sp.dma_start(Wv1_sb[:], Wv1.rearrange("(c p) n -> p c n", p=P)).then_inc(context_loaded, 16)

            def load(c, step, banks):
                if c.row is not None:
                    sp.wait_ge(sems["residual_kept"], c.at("residual_kept"))
                    sp.wait_ge(sems["pv_done"], c.at("pv_done"))
                sp.dma_start(x1[:], x[rows(c.ahead, 1)].rearrange("a (t p) d -> p (a t) d", p=P))\
                  .then_inc(sems["x_loaded"], 16)
                if c.row is not None:
                    sp.dma_start(V1[0:NK, :], v1_kept_hbm[rows(c.ahead * NK, NK), :])\
                      .then_inc(sems["v1_loaded"], 16)

            def context_keys(c, step, banks):
                for dst, src in ((Wq1_sb[:], Wq1.rearrange("(c p) n -> p c n", p=P)),
                                 (Wo1_sb[:], Wo1.rearrange("(c p) n -> p c n", p=P)),
                                 (U_sb[:], U), (V_sb[:], V), (SV_sb[:], SV),
                                 (gw1T_sb[:], gw1T.rearrange("(c p) n -> p c n", p=P)),
                                 (gw2T_sb[:], gw2T), (gb1_sb[:], gb1.rearrange("(p a) -> p a", a=1)),
                                 (gb2_sb[:], gb2.rearrange("(a n) -> a n", a=1).to_broadcast([P, E])),
                                 (qkb_sb[:], qkb),
                                 (vb_sb[:], vb.rearrange("(a n) -> a n", a=1).to_broadcast([P, D])),
                                 (ob_sb[:], ob.rearrange("(a n) -> a n", a=1).to_broadcast([P, D])),
                                 (expert_sb[:], expert)):
                    sp.dma_start(dst, src).then_inc(weights_loaded, 16)
                for dc in range(DC):
                    sp.dma_start(wm_ring[:, dc, :], WmT[QP, dc * P:(dc + 1) * P, :])\
                      .then_inc(sems[f"wm_loaded{dc}"], 16)

            def context_values(c, step, banks):
                for n, (first, end) in enumerate(CTX_TILES):
                    sp.wait_ge(sems["dve_evacuated"], c.at("dve_evacuated", n + 1))
                    sp.dma_start(v1_kept_hbm[first:end, :], V2[0:end - first, n % TT, :])\
                      .then_inc(sems["v1_kept"], 16)
                sp.wait_ge(sems["v1_kept"], 16 * len(CTX_TILES))
                sp.dma_start(V1[0:NK, :], v1_kept_hbm[0:NK, :]).then_inc(sems["v1_loaded"], 16)

            def weff(c, step, banks):
                nxt = (step[1] + 1) % 4
                if step[1] == OP and c.ahead is None:
                    return
                for dc in range(DC):
                    sp.wait_ge(sems["dve_evacuated"], c.at("dve_evacuated", dc + 1))
                    sp.dma_start(wm_ring[:, dc, :], WmT[nxt, dc * P:(dc + 1) * P, :])\
                      .then_inc(sems[f"wm_loaded{dc}"], 16)

            def duplicate(c, step, banks):
                if step[3] == 1:
                    sp.wait_ge(sems["hi_by_dve"], c.at("hi_by_dve", HJ // 2))
                    duplicate_keys(sp, step[2] % 2, 2)

            def move_shift(c, step, banks):
                for part in range(2):
                    done = ("shift_hi", "shift_lo")[part]
                    sp.wait_ge(sems[done], c.at(done, 1))
                    row = SHIFT_ROW + part
                    sp.dma_start(qs[row:row + 1, step[2] % 2, :, :].rearrange("p j (t n) -> p (j t) n", n=P)
                                 .bitcast(F32), shift[:, part, :].bitcast(F32))\
                      .then_inc(sems["shift_moved"], 16)

            def out2(c, step, banks):
                t = step[1]
                sp.wait_ge(sems["dve_evacuated"], c.at("dve_evacuated", 1))
                sp.dma_start(out[rows(c.row, 1), t * P:(t + 1) * P, :].rearrange("a p d -> p (a d)"),
                             kept[:, t, :]).then_inc(sems["out_stored"], 16)

            walk(sp, sp.Fori, {"load": load, "context_keys": context_keys,
                               "context_values": context_values, "weff": weff, "lo": duplicate,
                               "shift": move_shift,
                               "out2": out2})
            sp.wait_ge(sems["out_stored"], 16 * B * TT)

        @block.gpsimd
        def _(pool):
            for n, (what, value) in enumerate((
                    (ones[:], 1.0), (minus_half[:], -0.5), (negmax[:], 0.0),
                    (qs[MASK_ROW:MASK_ROW + 1, :, :, :].bitcast(F32), 1.0),
                    (ks[MASK_ROW:ROWS, :, :, :].bitcast(F32), 1.0),
                    (ks[MASK_ROW:MASK_ROW + 1, :, :, :].bitcast(F32), 0.0))):
                nc.gpsimd.memset(what, value).then_inc(consts_made, 1)
                pool.wait_ge(consts_made, n + 1)

            def inverse_deviation(c, step, banks):
                pool.wait_ge(sems["ln_step"], c.at("ln_step", TT + 1 + TT * (step[0] == "ln1")))
                if c.row is not None or step[0] == "ln2":
                    pool.wait_ge(sems["xhat_ready"], c.at("xhat_ready"))
                nc.gpsimd.tensor_tensor(rstd[:], vareps[:], minus_half[:], ALU.pow)\
                    .then_inc(sems["rstd_ready"], 1)
                if step[0] == "ln1" and c.row is not None:
                    pool.wait_ge(sems["bank_full"], c.at("bank_full"))
                    pool.wait_ge(sems["rstd_ready"], c.at("rstd_ready", 1))
                    if c.some("pool_settled"):
                        pool.wait_ge(sems["pool_settled"], c.at("pool_settled"))
                    nc.gpsimd.tensor_tensor(pool_carrier[:], minus_half[:, 0:1], minus_half[:, 0:1],
                                            ALU.add).then_inc(sems["pool_settled"], 1)
                    normalize(nc.gpsimd)

            def residual(c, step, banks):
                pool.wait_ge(sems["dve_evacuated"], c.at("dve_evacuated"))
                if c.row is None:
                    pool.wait_ge(weights_loaded, 16 * 13)
                else:
                    pool.wait_ge(sems["out_stored"], c.at("out_stored"))
                for t in range(TT):
                    nc.gpsimd.tensor_tensor(kept[:, t, :], x1[:, t, :], ob_sb[:], ALU.add)\
                        .then_inc(sems["residual_kept"], 1)

            def divide(c, step, banks):
                _, half, job = step
                pool.wait_ge(sems["copied"], c.at("copied", 2))
                n = S // pieces(job)
                for k in range(pieces(job)):
                    out_ = (ctx1T, ctx2T)[half][:, job, k * n:(k + 1) * n]
                    pool.wait_ge(sems["sum_inverted"], c.at("sum_inverted", k + 1))
                    nc.gpsimd.tensor_tensor(out_, out_, inv_sum[:, k * n:(k + 1) * n], ALU.mult)\
                        .then_inc(sems["normed"], 1)

            walk(pool, pool.Fori, {"finish": divide, "ln1": inverse_deviation, "ln2": inverse_deviation,
                                   "residual": residual})

        @block.scalar
        def _(act):
            def xpose(c, step, banks):
                for t in range(TT):
                    p, _ = banks.next("A", c.at, no_uses())
                    act.wait_ge(sems["bank_full"], c.at("bank_full", t + 1))
                    nc.scalar.activation(XT[:, :, t * P:(t + 1) * P],
                                         pj[:, p, :].rearrange("p (c n) -> p c n", c=DC),
                                         ACT.Copy).then_inc(sems["act_evacuated"], 1)

            def keys1_stack(c, step, banks):
                if c.row is None:
                    act.wait_ge(sems["dve_evacuated"], c.at("dve_evacuated"))
                    act.wait_ge(mask_step, B + 2)
                else:
                    act.wait_ge(sems["pv_done"], c.at("pv_done"))
                nc.scalar.activation(k1_hi[:], K1T[:, :, rows(c.ahead * NK, NK)], ACT.Copy)\
                    .then_inc(sems["keys1_hi"], 1)
                nc.scalar.activation(keys1[MASK_ROW:ROWS, :, :, :].rearrange("p c j k -> p (c j) k"),
                                     mask_rows[MASK_ROW:ROWS, rows(c.ahead, 1), :]
                                     .to_broadcast([ROWS - MASK_ROW, H, NKP]), ACT.Copy)\
                    .then_inc(sems["keys1_stacked"], 1)
                act.wait_ge(sems["keys1_hi"], c.at("keys1_hi", 1))
                for part in (0, 2, 1):
                    if part == 1:
                        act.wait_ge(sems["keys1_lo"], c.at("keys1_lo", 1))
                    for j in range(HJ):
                        src = (k1_lo if part == 1 else k1_hi)[j * DH:(j + 1) * DH]
                        nc.scalar.activation(keys1[part * DH:(part + 1) * DH, :, j, 0:NK], src.bitcast(F32),
                                             ACT.Copy).then_inc(sems["keys1_stacked"], 1)

            def exponentials(c, half, job, kt, done):
                keys = P if half == MIX else NK
                side = (kt if half == MIX else job) % 2
                read = kt - 1
                if c.some("pv_done", read):
                    act.wait_ge(sems["pv_done"], c.at("pv_done", read))
                for j in range(HJ):
                    act.wait_ge(sems["scoresT_full"], c.at("scoresT_full", done + j + 1))
                    nc.scalar.activation(probs[0:keys, side * HJ + j, :], scT[0:keys, j % 2, :],
                                         ACT.Exp, scale=SCALE).then_inc(sems["exp_done"], 1)

            def first(c, step, banks):
                if early_within(step):
                    exponentials(c, *early_within(step), 0, 0)

            def proj(c, step, banks):
                _, half, job, w, _, _ = step
                slot = job % 2
                first(c, step, banks)
                stack = (qs, ks)[w]
                p, _ = banks.next("L", c.at, no_uses())
                act.wait_ge(sems["bank_full"], c.at("bank_full", 1))
                for j in range(HJ if w == 0 else HJ // 2):
                    src = pj[j * DH:(j + 1) * DH, p, :]
                    dst = stack[0:DH, slot, j, :]
                    if half == MIX:
                        ins = nc.scalar.activation(dst, src, ACT.Identity,
                                                   bias=qkb_sb[j * DH:(j + 1) * DH, w, job:job + 1])
                    else:
                        ins = nc.scalar.activation(dst, src, ACT.Copy)
                    ins.then_inc(sems["hi_done"], 1)
                if w == 0:
                    act.wait_ge(sems["hi_done"], c.at("hi_done", HJ))
                    act.dma_start(qs[DH:2 * DH, slot, :, :].bitcast(F32), qs[0:DH, slot, :, :].bitcast(F32))\
                       .then_inc(sems[f"q_dup{slot}"], 16)
                else:
                    act.wait_ge(sems["hi_done"], c.at("hi_done", HJ // 2))
                    duplicate_keys(act, slot, 0)

            def attend(c, step, banks):
                _, half, job, _ = step
                for kt in range(1, TT):
                    exponentials(c, half, job, kt, HJ * (kt - 1))

            def finish(c, step, banks):
                _, half, job = step
                act.wait_ge(sems["pv_done"], c.at("pv_done", 1))
                if c.some("normed"):
                    act.wait_ge(sems["normed"], c.at("normed"))
                nc.scalar.activation(inv_sum[:], den[:, 0, :], ACT.Copy).then_inc(sems["copied"], 1)
                nc.scalar.activation((ctx1T, ctx2T)[half][:, job, :], acc[:, 0, :], ACT.Copy)\
                    .then_inc(sems["copied"], 1)

            def gate_hidden(c, step, banks):
                p, _ = banks.next("A", c.at, no_uses())
                if c.row is None:
                    act.wait_ge(weights_loaded, 16 * 13)
                act.wait_ge(sems["bank_full"], c.at("bank_full", 1))
                nc.scalar.activation(hidden[:], pj[:, p, 0:1], ACT.Relu, bias=gb1_sb[:], scale=1.0 / S)\
                    .then_inc(sems["act_evacuated"], 1)

            def gate_top(c, step, banks):
                act.wait_ge(sems["gate_step"], c.at("gate_step", 4))
                nc.scalar.activation(g[:, 1:2], g[:, 0:1], ACT.Exp).then_inc(sems["gate_exp"], 1)

            def pass_then_first(c, step, banks):
                for use in bank_uses(step):
                    banks.next(use, c.at, no_uses())
                first(c, step, banks)

            walk(act, act.Fori, {"xpose": xpose, "keys1": keys1_stack, "proj": proj, "first": first,
                                 "attend": attend,
                                 "weff": pass_then_first, "out2": pass_then_first,
                                 "finish": finish,
                                 "gate_hidden": gate_hidden, "gate_top": gate_top})

        @block.vector
        def _(dve):
            def settle(semaphore, value):
                dve.wait_ge(semaphore, value)
                nc.vector.memset(carrier[:], 0.0)

            dve.wait_ge(consts_loaded, 64)
            nc.vector.tensor_copy(lens_f[:], lens_i[:]).then_inc(mask_step, 1)
            dve.wait_ge(mask_step, 1)
            for b in range(B):
                nc.vector.tensor_scalar(valid[:, b, :], keypos_sb[:], lens_f[:, b:b + 1], None, ALU.is_lt)\
                    .then_inc(mask_step, 1)
            dve.wait_ge(mask_step, B + 1)
            nc.vector.tensor_scalar(mask_rows[MASK_ROW:ROWS, :, :], valid[MASK_ROW:ROWS, :, :],
                                    rowcoef_sb[MASK_ROW:ROWS, 0:1], rowcoef_sb[MASK_ROW:ROWS, 1:2],
                                    ALU.mult, ALU.add).then_inc(mask_step, 1)
            dve.wait_ge(mask_step, B + 2)

            def context_keys(c, step, banks):
                n = 0
                for co in range(DC):
                    for half in range(2):
                        p, _ = banks.next("D", c.at, no_uses())
                        n += 1
                        dve.wait_ge(sems["bank_full"], n)
                        nc.vector.tensor_tensor(
                            K1T[:, co, half * 4 * NK:(half + 1) * 4 * NK].rearrange("p (b k) -> p b k", k=NK),
                            pj[:, p, 0:4 * NK].rearrange("p (b k) -> p b k", k=NK),
                            valid[:, 4 * half:4 * half + 4, 0:NK], ALU.mult)\
                            .then_inc(sems["dve_evacuated"], 1)

            def context_values(c, step, banks):
                for k, (first, end) in enumerate(CTX_TILES):
                    p, _ = banks.next("D", c.at, no_uses())
                    dve.wait_ge(sems["bank_full"], c.at("bank_full", k + 1))
                    if k == TT:
                        dve.wait_ge(sems["v1_kept"], 16 * TT)
                    nc.vector.tensor_copy(V2[0:end - first, k % TT, :], pj[0:end - first, p, :])\
                        .then_inc(sems["dve_evacuated"], 1)

            def keys1_lo(c, step, banks):
                if c.row is None:
                    nc.vector.memset(keys1[0:3 * DH, :, :, NK:NKP].bitcast(F32), 0.0).then_inc(mask_step, 1)
                dve.wait_ge(sems["keys1_hi"], c.at("keys1_hi", 1))
                nc.vector.tensor_tensor(k1_lo[:], K1T[:, :, rows(c.ahead * NK, NK)], k1_hi[:].bitcast(F32),
                                        ALU.subtract).then_inc(sems["keys1_lo"], 1)

            def layernorm(c, step, banks):
                new = TT if step[0] == "ln1" else 0
                if new:
                    dve.wait_ge(sems["x_loaded"], c.at("x_loaded"))
                for t in range(new):
                    nc.vector.bn_stats(bn[:, t, :], x1[:, t, :]).then_inc(sems["ln_step"], 1)
                settle(sems["ln_step"], c.at("ln_step", new))
                for t in range(TT):
                    nc.vector.bn_aggr(meanvar[:, t, :], bn[:, t, :]).then_inc(sems["ln_step"], 1)
                dve.wait_ge(sems["ln_step"], c.at("ln_step", new + TT))
                nc.vector.tensor_scalar(vareps[:], meanvar[:, :, 1], EPS, None, ALU.add)\
                    .then_inc(sems["ln_step"], 1)
                if step[0] == "ln2" or c.row is None:
                    dve.wait_ge(sems["rstd_ready"], c.at("rstd_ready", 1))
                    if step[0] == "ln2":
                        dve.wait_ge(sems["bank_full"], c.at("bank_full"))
                    normalize(nc.vector)

            def reduce_scores(c, step, first, end):
                half, _, n0, _ = scores_within(step)
                for k in range(first, end):
                    n = n0 + k
                    dve.wait_ge(sems["scores_full"], c.at("scores_full", k + 1))
                    if half == MIX:
                        out_, in_ = negmax[:, n:n + 1], sc[:, n % 2, :]
                    else:
                        out_ = negmax[:, n:HJ * TT:TT]
                        in_ = sc[:, n % 2, 0:HJ * NKP].rearrange("p (j k) -> p j k", j=HJ)
                    nc.vector.tensor_reduce(out_, in_, AX.X, ALU.max, negate=True)\
                        .then_inc(sems["rowmax_done"], 1)

            def row_maxima(c, step, banks):
                if scores_within(step):
                    if c.row is None:
                        dve.wait_ge(consts_made, 6)
                    _, _, n0, n1 = scores_within(step)
                    reduce_scores(c, step, 0, n1 - n0)

            def xpose(c, step, banks):
                for use in bank_uses(step):
                    banks.next(use, c.at, no_uses())
                row_maxima(c, step, banks)

            projected = {}

            def proj(c, step, banks):
                p, _ = banks.next("L", c.at, no_uses())
                projected[step[1:4]] = p, c.here.get("hi_done", 0), c.here.get("bank_full", 0)
                row_maxima(c, step, banks)

            def lo_rows(c, step, banks):
                _, half, job, w = step
                slot = job % 2
                stack = (qs, ks)[w]
                p, hi_before, bank_before = projected[step[1:4]]
                at = (2 * DH, DH)[w]

                def of_head(j):
                    src = pj[j * DH:(j + 1) * DH, p, :]
                    return src, qkb_sb[j * DH:(j + 1) * DH, w, job:job + 1] if half == MIX else 0.0

                by_act = HJ if w == 0 else HJ // 2
                for j in range(by_act, HJ):
                    dve.wait_ge(sems["bank_full"], c.at("bank_full", bank_before - c.here["bank_full"] + 1))
                    src, bias = of_head(j)
                    nc.vector.tensor_scalar(stack[0:DH, slot, j, :], src, bias, None, ALU.add)\
                        .then_inc(sems["hi_by_dve"], 1)
                for j in range(HJ):
                    if j < by_act:
                        dve.wait_ge(sems["hi_done"], c.at("hi_done", hi_before - c.here["hi_done"] + j + 1))
                    else:
                        dve.wait_ge(sems["hi_by_dve"], c.at("hi_by_dve", j - by_act + 1))
                    src, bias = of_head(j)
                    nc.vector.scalar_tensor_tensor(stack[at:at + DH, slot, j, :], src, bias,
                                                   stack[0:DH, slot, j, :].bitcast(F32),
                                                   ALU.add, ALU.subtract)\
                        .then_inc(sems["lo_evacuated" if j == HJ - 1 else "lo_step"], 1)

            def shift_parts(c, step, banks):
                dve.wait_ge(sems["shift_turned"], c.at("shift_turned", 1))
                if c.some("shift_moved"):
                    dve.wait_ge(sems["shift_moved"], c.at("shift_moved"))
                nc.vector.tensor_copy(shift[:, 0, :], sc[0:HJ * TT, 0, 0:P]).then_inc(sems["shift_hi"], 1)
                dve.wait_ge(sems["shift_hi"], c.at("shift_hi", 1))
                nc.vector.tensor_tensor(shift[:, 1, :], sc[0:HJ * TT, 0, 0:P], shift[:, 0, :].bitcast(F32),
                                        ALU.subtract).then_inc(sems["shift_lo"], 1)

            def invert(c, step, banks):
                dve.wait_ge(sems["copied"], c.at("copied", 1))
                n = S // pieces(step[2])
                for k in range(pieces(step[2])):
                    nc.vector.reciprocal(inv_sum[:, k * n:(k + 1) * n], inv_sum[:, k * n:(k + 1) * n])\
                        .then_inc(sems["sum_inverted"], 1)

            def scale_v(c, p, k):
                dve.wait_ge(sems["bank_full"], c.at("bank_full", k))
                nc.vector.tensor_scalar(vs[:, p % 2, :], V_sb[:, p, :], g[:, 10 + p:11 + p], None, ALU.mult)\
                    .then_inc(sems["vs_ready"], 1)

            def weff(c, step, banks):
                p = step[1]
                if p != OP:
                    scale_v(c, p + 1, 0)
                dst = Wvo if p in (VP, OP) else Wqk[:, p]
                for dc in range(DC):
                    b, _ = banks.next("D", c.at, no_uses())
                    dve.wait_ge(sems[f"wm_loaded{dc}"], c.at(f"wm_loaded{dc}", 16))
                    dve.wait_ge(sems["bank_full"], c.at("bank_full", dc + 1))
                    nc.vector.tensor_tensor(dst[:, dc, :], pj[:, b, :], wm_ring[:, dc, :], ALU.add)\
                        .then_inc(sems["dve_evacuated"], 1)

            def vproj(c, step, banks):
                for t in range(TT):
                    p, _ = banks.next("D", c.at, no_uses())
                    reduce_scores(c, step, scores_by((DC - 1) * t), scores_by((DC - 1) * (t + 1)))
                    dve.wait_ge(sems["bank_full"], c.at("bank_full", t + 1))
                    nc.vector.tensor_tensor(V2[:, t, :], pj[:, p, :], vb_sb[:], ALU.add)\
                        .then_inc(sems["dve_evacuated"], 1)

            def out1(c, step, banks):
                for t in range(TT):
                    p, _ = banks.next("D", c.at, no_uses())
                    dve.wait_ge(sems["bank_full"], c.at("bank_full", t + 1))
                    nc.vector.tensor_tensor(x1[:, t, :], pj[:, p, :], x1[:, t, :], ALU.add)\
                        .then_inc(sems["dve_evacuated"], 1)
                    dve.wait_ge(sems["dve_evacuated"], c.at("dve_evacuated", t + 1))
                    nc.vector.bn_stats(bn[:, t, :], x1[:, t, :]).then_inc(sems["ln_step"], 1)

            def out2(c, step, banks):
                t = step[1]
                p, _ = banks.next("D", c.at, no_uses())
                dve.wait_ge(sems["residual_kept"], c.at("residual_kept"))
                dve.wait_ge(sems["bank_full"], c.at("bank_full", 1))
                nc.vector.tensor_tensor(kept[:, t, :], pj[:, p, :], kept[:, t, :], ALU.add)\
                    .then_inc(sems["dve_evacuated"], 1)

            def pool_tokens(c, step, banks):
                for t in range(TT):
                    dve.wait_ge(sems["act_evacuated"], c.at("act_evacuated", t + 1 - TT))
                    nc.vector.tensor_reduce(tile_sums[:, :, t:t + 1], XT[:, :, t * P:(t + 1) * P], AX.X,
                                            ALU.add).then_inc(sems["gate_step"], 1)
                dve.wait_ge(sems["gate_step"], c.at("gate_step", TT))
                nc.vector.tensor_reduce(pooled[:], tile_sums[:], AX.X, ALU.add).then_inc(sems["gate_step"], 1)

            def gate_hidden(c, step, banks):
                banks.next("A", c.at, no_uses())
                dve.wait_ge(sems["act_evacuated"], c.at("act_evacuated", 1))
                nc.vector.tensor_scalar(hiddenB[:], ones[:], hidden[:, 0:1], None, ALU.mult)\
                    .then_inc(sems["gate_step"], 1)

            def gate_top(c, step, banks):
                p, _ = banks.next("D", c.at, no_uses())
                n = 0

                def step_done(ins):
                    nonlocal n
                    n += 1
                    ins.then_inc(sems["gate_step"], 1)
                    wait = settle if n == 1 else dve.wait_ge
                    wait(sems["gate_step"], c.at("gate_step", n))

                dve.wait_ge(sems["bank_full"], c.at("bank_full", 1))
                nc.vector.tensor_tensor(logits[:], pj[:, p, 0:E], gb2_sb[:], ALU.add)\
                    .then_inc(sems["dve_evacuated"], 1)
                settle(sems["dve_evacuated"], c.at("dve_evacuated", 1))
                step_done(nc.vector.max(top[:], logits[:]))
                step_done(nc.vector.max_index(top_at[:], top[:], logits[:]))
                step_done(nc.vector.tensor_copy(g[:, 2:4], top_at[:, 0:2]))
                step_done(nc.vector.tensor_tensor(g[:, 0:1], top[:, 1:2], top[:, 0:1], ALU.subtract))
                dve.wait_ge(sems["gate_exp"], c.at("gate_exp", 1))
                step_done(nc.vector.tensor_scalar(g[:, 4:5], g[:, 1:2], 1.0, None, ALU.add))
                step_done(nc.vector.reciprocal(g[:, 5:6], g[:, 4:5]))
                step_done(nc.vector.tensor_tensor(g[:, 6:7], g[:, 5:6], g[:, 1:2], ALU.mult))
                step_done(nc.vector.tensor_scalar(sel[:], g[:, 2:4], expert_sb[:, 0:1], None, ALU.is_equal))
                step_done(nc.vector.tensor_tensor(g[:, 7:9], sel[:], g[:, 5:7], ALU.mult))
                step_done(nc.vector.tensor_tensor(g[:, 9:10], g[:, 7:8], g[:, 8:9], ALU.add))
                step_done(nc.vector.tensor_scalar(g[:, 10:14], SV_sb[:], g[:, 9:10], None, ALU.mult))
                scale_v(c, QP, 0)

            walk(dve, dve.Fori, {"context_keys": context_keys, "context_values": context_values,
                                  "keys1": keys1_lo, "ln1": layernorm,
                                 "ln2": layernorm, "proj": proj, "lo": lo_rows,
                                 "scores": row_maxima, "xpose": xpose,
                                 "shift": shift_parts, "attend": row_maxima, "finish": invert,
                                 "pooled": pool_tokens, "weff": weff, "vproj": vproj, "out1": out1,
                                 "out2": out2, "gate_hidden": gate_hidden, "gate_top": gate_top})

        @block.tensor
        def _(pe):
            pe.wait_ge(consts_loaded, 64)
            pe.wait_ge(consts_made, 6)

            def take(c, banks, engine, used):
                p, waits = banks.next(engine, c.at, used)
                for name, value in waits:
                    pe.wait_ge(sems[name], value)
                return p

            def context_keys(c, step, banks):
                used = no_uses()
                pe.wait_ge(context_loaded, 48)
                for co in range(DC):
                    for half in range(2):
                        p = take(c, banks, "D", used)
                        for dc in range(DC):
                            mm = nc.tensor.matmul(pj[:, p, 0:4 * NK], Wk1_sb[:, dc, co * P:(co + 1) * P],
                                                  ctxT_sb[:, dc, half * 4 * NK:(half + 1) * 4 * NK],
                                                  start=(dc == 0), stop=(dc == DC - 1))
                        mm.then_inc(sems["bank_full"], 1)

            def context_values(c, step, banks):
                used = no_uses()
                for first, end in CTX_TILES:
                    p = take(c, banks, "D", used)
                    for dc in range(DC):
                        mm = nc.tensor.matmul(pj[0:end - first, p, :], ctxT_sb[:, dc, first:end],
                                              Wv1_sb[:, dc, :], start=(dc == 0), stop=(dc == DC - 1))
                    mm.then_inc(sems["bank_full"], 1)

            def xpose(c, step, banks):
                used = no_uses()
                for t in range(TT):
                    p = take(c, banks, "A", used)
                    pe.wait_ge(sems["xhat_ready"], c.at("xhat_ready", t + 1 - TT))
                    for dc in range(DC):
                        mm = nc.tensor.transpose(pj[:, p, dc * P:(dc + 1) * P], xhat[:, t, dc * P:(dc + 1) * P],
                                                 ident_sb[:])
                    mm.then_inc(sems["bank_full"], 1)
                    if scores_within(step):
                        scores(c, step, PLACES[MIX][t], PLACES[MIX][t + 1])

            stacked = {}

            def stacks_ready(c, half, job):
                slot = job % 2
                pe.wait_ge(sems["lo_evacuated"],
                           c.at("lo_evacuated", stacked[half, job] - c.here["lo_evacuated"]))
                pe.wait_ge(sems[f"q_dup{slot}"], c.at(f"q_dup{slot}"))
                if half == CROSS:
                    pe.wait_ge(sems["keys1_stacked"], c.at("keys1_stacked"))
                    if c.row is None:
                        pe.wait_ge(mask_step, B + 3)
                else:
                    pe.wait_ge(sems[f"k_dup{slot}_01"], c.at(f"k_dup{slot}_01"))

            def scores(c, step, first, end):
                if not scores_within(step):
                    return
                half, job, n0, n1 = scores_within(step)
                slot = job % 2
                for k in range(first, end):
                    n = n0 + k
                    if n == 0:
                        stacks_ready(c, half, job)
                        if c.some("shift_lo"):
                            pe.wait_ge(sems["shift_lo"], c.at("shift_lo"))
                    if c.some("rowmax_done", k - 1):
                        pe.wait_ge(sems["rowmax_done"], c.at("rowmax_done", k - 1))
                    if half == MIX:
                        j, t = n // TT, n % TT
                        if n == 2 * TT:
                            pe.wait_ge(sems[f"k_dup{slot}_23"], c.at(f"k_dup{slot}_23"))
                        nc.tensor.matmul(sc[:, n % 2, :], qs[0:3 * DH, slot, j, t * P:(t + 1) * P],
                                         ks[0:3 * DH, slot, j, :], start=True, stop=True)\
                            .then_inc(sems["scores_full"], 1)
                    else:
                        for j in range(HJ):
                            mm = nc.tensor.matmul(sc[:, n % 2, j * NKP:(j + 1) * NKP],
                                                  qs[0:MASK_ROW + 1, slot, j, n * P:(n + 1) * P],
                                                  keys1[0:MASK_ROW + 1, job, j, :], start=True, stop=True)
                        mm.then_inc(sems["scores_full"], 1)

            def scores_transposed(c, half, job, kt, j, done):
                slot = job % 2
                if kt == 0 and j == 0:
                    pe.wait_ge(sems["shift_moved"], c.at("shift_moved"))
                if c.some("exp_done", done - 1):
                    pe.wait_ge(sems["exp_done"], c.at("exp_done", done - 1))
                keys = P if half == MIX else NK
                lhsT = (ks[0:ROWS, slot, j, kt * P:(kt + 1) * P] if half == MIX
                        else keys1[0:ROWS, job, j, 0:NK])
                nc.tensor.matmul(scT[0:keys, j % 2, :], lhsT, qs[0:ROWS, slot, j, :],
                                 start=True, stop=True).then_inc(sems["scoresT_full"], 1)

            def scores_alone(c, step, banks):
                scores(c, step, 0, step[1][3])

            def early_scores(c, step, j):
                if early_within(step):
                    scores_transposed(c, *early_within(step), 0, j, j)

            def first(c, step, banks):
                for j in range(HJ):
                    early_scores(c, step, j)

            def proj(c, step, banks):
                _, half, job, w, _, _ = step
                if c.row is None:
                    pe.wait_ge(weights_loaded, 16 * 13)
                pe.wait_ge(sems["act_evacuated"], c.at("act_evacuated"))
                if half == MIX and job == 0:
                    pe.wait_ge(sems["dve_evacuated"], c.at("dve_evacuated", (w - 2) * DC))
                stacked[half, job] = c.here.get("lo_evacuated", 0) + 1
                p = take(c, banks, "L", no_uses())
                W = Wq1_sb if half == CROSS else Wqk[:, w]
                for dc in range(DC):
                    mm = nc.tensor.matmul(pj[:, p, :], W[:, dc, job * P:(job + 1) * P], XT[:, dc, :],
                                          start=(dc == 0), stop=(dc == DC - 1))
                    if dc == DC - 1:
                        mm.then_inc(sems["bank_full"], 1)
                    early_scores(c, step, dc)
                    if step[-1]:
                        places = PLACES[step[-1][0]]
                        scores(c, step, places[dc], places[dc + 1])

            def turn_shift(c, step, banks):
                pe.wait_ge(sems["rowmax_done"], c.at("rowmax_done"))
                nc.tensor.transpose(sc[:, 0, 0:P], negmax[:], ident_sb[:]).then_inc(sems["shift_turned"], 1)

            def p_times_v(half, job, kt, to):
                keys, key_tiles = (P, TT) if half == MIX else (NK, 1)
                side = (kt if half == MIX else job) % 2
                for j in range(HJ):
                    head = (job * HJ + j) * DH
                    lhsT = (ones[0:keys, 0:DH] if to is den else
                            V2[:, kt, head:head + DH] if half == MIX else V1[0:NK, head:head + DH])
                    mm = nc.tensor.matmul(to[j * DH:(j + 1) * DH, 0, :], lhsT,
                                          probs[0:keys, side * HJ + j, :],
                                          start=(kt == 0), stop=(kt == key_tiles - 1))
                if to is den:
                    mm.then_inc(sems["pv_done"], 1)

            def attend(c, step, banks):
                _, half, job, within = step
                tiles = within[3] - within[2] if within else 0
                per_key_tile, skipped = 6, 5 if tiles > TT else 12
                places = per_key_tile * (TT - 1) - skipped
                filled, place = 0, 0

                def scores_between():
                    nonlocal filled, place
                    place += 1
                    until = max(0, -(-tiles * (place - skipped) // places))
                    if until > filled:
                        scores(c, step, filled, until)
                        filled = until

                for kt in range(1, TT):
                    done = HJ * (kt - 1)
                    scores_transposed(c, half, job, kt, 0, done)
                    scores_between()
                    scores_transposed(c, half, job, kt, 1, done + 1)
                    scores_between()
                    pe.wait_ge(sems["exp_done"], c.at("exp_done", done))
                    if kt == 1:
                        pe.wait_ge(sems["copied"], c.at("copied"))
                    p_times_v(half, job, kt - 1, acc)
                    scores_between()
                    if kt == 1:
                        p_times_v(half, job, kt - 1, den)
                    scores_transposed(c, half, job, kt, 2, done + 2)
                    scores_between()
                    scores_transposed(c, half, job, kt, 3, done + 3)
                    scores_between()
                    if kt > 1:
                        p_times_v(half, job, kt - 1, den)
                    scores_between()

            finishing = {}

            def finish(c, step, banks):
                _, half, job = step
                finishing[half, job] = c.here.get("normed", 0)
                pe.wait_ge(sems["exp_done"], c.at("exp_done"))
                if half == CROSS:
                    pe.wait_ge(sems["v1_loaded"], c.at("v1_loaded"))
                    if c.some("copied"):
                        pe.wait_ge(sems["copied"], c.at("copied"))
                for to in (acc, den):
                    p_times_v(half, job, TT - 1 if half == MIX else 0, to)

            def weff(c, step, banks):
                p = step[1]
                used = no_uses()
                pe.wait_ge(sems["vs_ready"], c.at("vs_ready"))
                for dc in range(DC):
                    b = take(c, banks, "D", used)
                    nc.tensor.matmul(pj[:, b, :], vs[:, p % 2, dc * P:(dc + 1) * P], U_sb[:, p, :],
                                     start=True, stop=True).then_inc(sems["bank_full"], 1)
                    early_scores(c, step, dc)

            def vproj(c, step, banks):
                used = no_uses()
                pe.wait_ge(sems["act_evacuated"], c.at("act_evacuated"))
                pe.wait_ge(sems["dve_evacuated"], c.at("dve_evacuated"))
                for t in range(TT):
                    p = take(c, banks, "D", used)
                    for dc in range(DC):
                        mm = nc.tensor.matmul(pj[:, p, :], XT[:, dc, t * P:(t + 1) * P], Wvo[:, dc, :],
                                              start=(dc == 0), stop=(dc == DC - 1))
                        if dc < DC - 1:
                            place = (DC - 1) * t + dc
                            scores(c, step, scores_by(place), scores_by(place + 1))
                    mm.then_inc(sems["bank_full"], 1)

            def project_out(c, step, banks, used, srcT, W, t):
                p = take(c, banks, "D", used)
                for dc in range(DC):
                    mm = nc.tensor.matmul(pj[:, p, :], srcT[:, dc, t * P:(t + 1) * P], W[:, dc, :],
                                          start=(dc == 0), stop=(dc == DC - 1))
                    if dc == DC - 1:
                        mm.then_inc(sems["bank_full"], 1)
                    early_scores(c, step, dc)

            def out1(c, step, banks):
                used = no_uses()
                for t in range(TT):
                    pe.wait_ge(sems["normed"], c.at("normed", t + 1 - TT))
                    project_out(c, step, banks, used, ctx1T, Wo1_sb, t)

            def out2(c, step, banks):
                pe.wait_ge(sems["normed"], c.at("normed", finishing[MIX, DC - 1] + step[1] + 1
                                                - c.here["normed"]))
                if step[1] == 0:
                    pe.wait_ge(sems["dve_evacuated"], c.at("dve_evacuated"))
                project_out(c, step, banks, no_uses(), ctx2T, Wvo, step[1])

            def gate_hidden(c, step, banks):
                p = take(c, banks, "A", no_uses())
                pe.wait_ge(sems["gate_step"], c.at("gate_step"))
                for dc in range(DC):
                    mm = nc.tensor.matmul(pj[:, p, 0:1], gw1T_sb[:, dc, :], pooled[:, dc:dc + 1],
                                          start=(dc == 0), stop=(dc == DC - 1))
                mm.then_inc(sems["bank_full"], 1)

            def gate_top(c, step, banks):
                p = take(c, banks, "D", no_uses())
                pe.wait_ge(sems["gate_step"], c.at("gate_step"))
                nc.tensor.matmul(pj[:, p, 0:E], hiddenB[:], gw2T_sb[:], start=True, stop=True)\
                    .then_inc(sems["bank_full"], 1)

            walk(pe, pe.Fori, {"context_keys": context_keys, "context_values": context_values,
                                "xpose": xpose, "proj": proj, "scores": scores_alone,
                               "shift": turn_shift, "first": first, "attend": attend,
                               "finish": finish, "weff": weff, "vproj": vproj,
                               "out1": out1, "out2": out2, "gate_hidden": gate_hidden,
                               "gate_top": gate_top})


def kernel(x, ctx_1024, _lenS2, L0_xattn_Wq, L0_xattn_Wk, L0_xattn_Wv, L0_xattn_Wo, **ffn):
    import numpy as np
    import concourse.bacc as bacc
    from concourse.bass_utils import run_bass_kernel_spmd

    w = {k.removeprefix("L0_ffn_"): np.asarray(v) for k, v in ffn.items()}
    at = np.arange(P)
    rowcoef = np.zeros((P, 2), np.float32)
    rowcoef[MASK_ROW] = (-MASKED, MASKED)
    rowcoef[SHIFT_ROW:ROWS] = (0.0, 1.0)
    keypos = np.full((P, NKP), 1e9, np.float32)
    keypos[:, :NK] = np.arange(NK)
    ins = {
        "x": x,
        "ctxT": np.asarray(ctx_1024).reshape(B * NK, D).T,
        "lens": np.asarray(_lenS2),
        "Wq1": L0_xattn_Wq, "Wk1": L0_xattn_Wk, "Wv1": L0_xattn_Wv, "Wo1": L0_xattn_Wo,
        "gw1T": w["gw1"].T, "gb1": w["gb1"], "gw2T": w["gw2"].T, "gb2": w["gb2"],
        "WmT": np.stack([w[p + "Wm"].T for p in "qkvo"]),
        "U": np.stack([w[p + "U"].transpose(0, 2, 1).reshape(E * R, D) for p in "qkvo"], 1),
        "V": np.stack([w[p + "V"].reshape(E * R, D) for p in "qkvo"], 1),
        "SV": np.stack([w[p + "S"].reshape(E * R) for p in "qkvo"], 1),
        "qkb": np.stack([w[p + "b"].reshape(DC, P).T for p in "qk"], 1), "vb": w["vb"], "ob": w["ob"],
        "ident": np.eye(P, dtype=np.float32),
        "keypos": keypos,
        "expert": (at // R).astype(np.float32).reshape(P, 1),
        "rowcoef": rowcoef,
    }
    nc = bacc.Bacc("TRN2", target_bir_lowering=False, num_devices=1)
    arrays, aps = {}, {}
    for name, a in ins.items():
        a = np.ascontiguousarray(a)
        arrays[f"in_{name}"] = a
        aps[name] = nc.dram_tensor(f"in_{name}", a.shape, mybir.dt.from_np(a.dtype), kind="ExternalInput").ap()
    out = nc.dram_tensor("out", (B, S, D), F32, kind="ExternalOutput").ap()
    v1_kept_hbm = nc.dram_tensor("v1_kept_hbm", (B * NK, D), F32, kind="Internal").ap()
    cross_and_mixture_attention(nc, **aps, out=out, v1_kept_hbm=v1_kept_hbm)
    return run_bass_kernel_spmd(nc, [arrays], core_ids=[0]).results[0]["out"]
```
